# Optimizing a Trainium2 kernel written in Bass

```python
import numpy as np
import jax
import jax.numpy as jnp

def _softmax(x, axis=-1):
    return jax.nn.softmax(x, axis=axis)

def _gelu(x):
    return jax.nn.gelu(x, approximate=True)

def _silu(x):
    return jax.nn.silu(x)

def _sigmoid(x):
    return jax.nn.sigmoid(x)

def _layernorm(x, axis=-1, eps=1e-05):
    m = jnp.mean(x, axis=axis, keepdims=True)
    v = jnp.var(x, axis=axis, keepdims=True)
    return (x - m) / jnp.sqrt(v + eps)

def _scatter_add(tgt, idx, src, axis=0):
    return tgt.at[idx].add(src)

def _segment_sum(src, seg, n):
    return jax.ops.segment_sum(src, seg, n)
kernel_name = 'mk_adaln_ffn_d2_seqx_r8_4b042a'

def setup_inputs(seed: int=0):
    np.random.seed(seed)
    _w = jnp.asarray

    def _rec_inputs():
        import jax
        import jax.numpy as jnp
        _rk = jax.random.key(seed)
        x = 0.0001734 + 0.8201 * jax.random.normal(jax.random.fold_in(_rk, 1), (64, 32, 512), jnp.float32)
        _lenS = 32 - jax.random.randint(jax.random.fold_in(_rk, 7), (64,), 0, max(1, 32 // 4) + 1, jnp.int32)
        _lenS2 = 32 - jax.random.randint(jax.random.fold_in(_rk, 8), (64,), 0, max(1, 32 // 4) + 1, jnp.int32)
        itok_B_0_7 = jax.random.randint(jax.random.fold_in(_rk, 11), (64,), 0, 8, jnp.int32)
        itok_B_2182_4065 = jax.random.randint(jax.random.fold_in(_rk, 13), (64,), 2182, 4066, jnp.int32)
        itok_B_8_3872 = jax.random.randint(jax.random.fold_in(_rk, 14), (64,), 8, 3873, jnp.int32)
        return (x, itok_B_0_7, itok_B_2182_4065, itok_B_8_3872, _lenS)
    x, itok_B_0_7, itok_B_2182_4065, itok_B_8_3872, _lenS = _rec_inputs()

    def _L0_cond_setup():
        import jax, jax.numpy as jnp
        import numpy as np
        SESSION_CHANNELS = [128, 160, 192, 224, 240, 248, 252, 32]
        N_SESS = len(SESSION_CHANNELS)
        B, MAX_C, MAX_T = (16, 32, 512)
        HID, N_SRC = (64, 32)
        key = jax.random.key(seed)
        ks = jax.random.split(key, 7)
        session_ids = jax.random.randint(ks[0], (B,), 0, N_SESS)
        chan_table = jnp.asarray(SESSION_CHANNELS)
        channel_counts = chan_table[session_ids]
        seq_lens = jax.random.randint(ks[1], (B,), MAX_T // 2, MAX_T + 1)
        x = jax.random.normal(ks[2], (B, MAX_C, MAX_T), jnp.float32)
        cmask = (jnp.arange(MAX_C)[None, :] < channel_counts[:, None]).astype(x.dtype)
        tmask = (jnp.arange(MAX_T)[None, :] < seq_lens[:, None]).astype(x.dtype)
        x = x * cmask[:, :, None] * tmask[:, None, :]
        lim1 = 1.0 / np.sqrt(MAX_C)
        W_sess = jax.random.uniform(ks[3], (N_SESS, MAX_C, HID), jnp.float32, -lim1, lim1)
        b_sess = jax.random.uniform(ks[4], (N_SESS, HID), jnp.float32, -lim1, lim1)
        lim2 = 1.0 / np.sqrt(HID)
        W2 = jax.random.uniform(ks[5], (HID, N_SRC), jnp.float32, -lim2, lim2)
        b2 = jax.random.uniform(ks[6], (N_SRC,), jnp.float32, -lim2, lim2)
        return dict(x=x, session_ids=session_ids, channel_counts=channel_counts, seq_lens=seq_lens, W_sess=W_sess, b_sess=b_sess, W2=W2, b2=b2)
    _L0_cond_all = _L0_cond_setup()
    _L0_cond_in = {k: v for k, v in _L0_cond_all.items() if k in ('W_sess', 'b_sess', 'W2', 'b2')}
    del _L0_cond_all

    def _L0_ffn_setup():
        import jax, jax.numpy as jnp
        import numpy as np
        NUM_EXPERTS = 8
        TOP_K = 2
        RANK = 16
        LORA_ALPHA = 32
        SCALING = LORA_ALPHA / RANK
        key = jax.random.key(seed)
        ks = jax.random.split(key, 6)
        B, S, D_IN, D_OUT = (4, 256, 512, 512)
        x = jax.random.normal(ks[0], (B, S, D_IN), dtype=jnp.float32)
        W_base = jax.random.normal(ks[1], (D_OUT, D_IN), dtype=jnp.float32) * 0.02
        b_base = jax.random.normal(ks[2], (D_OUT,), dtype=jnp.float32) * 0.02
        W_router = jax.random.normal(ks[3], (NUM_EXPERTS, D_IN), dtype=jnp.float32) * 0.02
        A = jax.random.normal(ks[4], (NUM_EXPERTS, RANK, D_IN), dtype=jnp.float32) * 0.02
        Bm = jax.random.normal(ks[5], (D_OUT, RANK), dtype=jnp.float32) * 0.02
        Bm = jnp.broadcast_to(Bm, (NUM_EXPERTS, D_OUT, RANK)) * jnp.arange(1, NUM_EXPERTS + 1, dtype=jnp.float32)[:, None, None] * 0.2
        return {'x': x, 'W_base': W_base, 'b_base': b_base, 'W_router': W_router, 'A': A, 'B': Bm}
    _L0_ffn_all = _L0_ffn_setup()
    _L0_ffn_in = {k: v for k, v in _L0_ffn_all.items() if k in ('W_base', 'b_base', 'W_router', 'A', 'B')}
    del _L0_ffn_all

    def _L1_cond_setup():
        import math
        import jax, jax.numpy as jnp
        import numpy as np
        H, N, B, L = (32, 64, 16, 512)
        DT_MIN, DT_MAX = (0.001, 0.1)

        def _get_kernel(log_dt, C, log_A_real, A_imag, length):
            Cc = C[..., 0] + 1j * C[..., 1]
            dt = jnp.exp(log_dt)
            A = -jnp.exp(log_A_real) + 1j * A_imag
            dtA = A * dt[:, None]
            P = dtA[:, :, None] * jnp.arange(length, dtype=jnp.float32)
            Cs = Cc * (jnp.exp(dtA) - 1.0) / A
            K = 2.0 * jnp.einsum('hn,hnl->hl', Cs, jnp.exp(P)).real
            return K
        key = jax.random.key(seed)
        ks = jax.random.split(key, 6)
        u = jax.random.normal(ks[0], (B, H, L), dtype=jnp.float32)
        length = jax.random.randint(ks[1], (B,), 0, L)
        log_dt = jax.random.uniform(ks[2], (H,), dtype=jnp.float32) * (math.log(DT_MAX) - math.log(DT_MIN)) + math.log(DT_MIN)
        C = jax.random.normal(ks[3], (H, N, 2), dtype=jnp.float32)
        log_A_real = jnp.log(0.5 * jnp.ones((H, N), dtype=jnp.float32))
        A_imag = math.pi * jnp.broadcast_to(jnp.arange(N, dtype=jnp.float32), (H, N))
        D = jax.random.normal(ks[4], (H,), dtype=jnp.float32)
        return {'u': u, 'length': length, 'log_dt': log_dt, 'C': C, 'log_A_real': log_A_real, 'A_imag': A_imag, 'D': D}
    _L1_cond_all = _L1_cond_setup()
    _L1_cond_in = {k: v for k, v in _L1_cond_all.items() if k in ('log_dt', 'C', 'log_A_real', 'A_imag', 'D')}
    del _L1_cond_all

    def _L1_ffn_setup():
        import jax, jax.numpy as jnp
        import numpy as np
        B, L, H, Dh, M = (4, 256, 16, 32, 128)
        D = H * Dh
        key = jax.random.key(seed)
        kx, ku, kd, kp = jax.random.split(key, 4)
        x = jax.random.normal(kx, (B, L, D), dtype=jnp.float32)
        up = jax.random.normal(ku, (H, Dh, M), dtype=jnp.float32)
        down = jax.random.normal(kd, (H, M, Dh), dtype=jnp.float32)
        perm = jax.random.permutation(kp, D)
        return {'x': x, 'up': up, 'down': down, 'perm': perm}
    _L1_ffn_all = _L1_ffn_setup()
    _L1_ffn_in = {k: v for k, v in _L1_ffn_all.items() if k in ('up', 'down', 'perm')}
    del _L1_ffn_all
    return {'x': x, 'itok_B_0_7': itok_B_0_7, 'itok_B_2182_4065': itok_B_2182_4065, 'itok_B_8_3872': itok_B_8_3872, '_lenS': _lenS, 'L0_cond_W_sess': _L0_cond_in['W_sess'], 'L0_cond_b_sess': _L0_cond_in['b_sess'], 'L0_cond_W2': _L0_cond_in['W2'], 'L0_cond_b2': _L0_cond_in['b2'], 'L0_ffn_W_base': _L0_ffn_in['W_base'], 'L0_ffn_b_base': _L0_ffn_in['b_base'], 'L0_ffn_W_router': _L0_ffn_in['W_router'], 'L0_ffn_A': _L0_ffn_in['A'], 'L0_ffn_B': _L0_ffn_in['B'], 'L1_cond_log_dt': _L1_cond_in['log_dt'], 'L1_cond_C': _L1_cond_in['C'], 'L1_cond_log_A_real': _L1_cond_in['log_A_real'], 'L1_cond_A_imag': _L1_cond_in['A_imag'], 'L1_cond_D': _L1_cond_in['D'], 'L1_ffn_up': _L1_ffn_in['up'], 'L1_ffn_down': _L1_ffn_in['down'], 'L1_ffn_perm': _L1_ffn_in['perm']}

def reference(x, itok_B_0_7, itok_B_2182_4065, itok_B_8_3872, _lenS, L0_cond_W_sess, L0_cond_b_sess, L0_cond_W2, L0_cond_b2, L0_ffn_W_base, L0_ffn_b_base, L0_ffn_W_router, L0_ffn_A, L0_ffn_B, L1_cond_log_dt, L1_cond_C, L1_cond_log_A_real, L1_cond_A_imag, L1_cond_D, L1_ffn_up, L1_ffn_down, L1_ffn_perm):
    import jax
    import jax.numpy as jnp

    def _L0_cond_ref(x, session_ids, channel_counts, seq_lens, W_sess, b_sess, W2, b2):
        import jax, jax.numpy as jnp
        import numpy as np
        SESSION_CHANNELS = [128, 160, 192, 224, 240, 248, 252, 32]
        N_SESS = len(SESSION_CHANNELS)
        B, MAX_C, MAX_T = (16, 32, 512)
        HID, N_SRC = (64, 32)
        cmask = (jnp.arange(x.shape[1])[None, :] < channel_counts[:, None]).astype(x.dtype)
        xm = x * cmask[:, :, None]
        W = W_sess[session_ids]
        b = b_sess[session_ids]
        h = jnp.einsum('bct,bch->bht', xm, W) + b[:, :, None]
        h = jax.nn.gelu(h, approximate=False)
        out = jnp.einsum('bht,hs->bst', h, W2) + b2[None, :, None]
        tmask = (jnp.arange(x.shape[2])[None, :] < seq_lens[:, None]).astype(x.dtype)
        return out * tmask[:, None, :]

    def _L0_ffn_ref(x, W_base, b_base, W_router, A, B):
        import jax, jax.numpy as jnp
        import numpy as np
        NUM_EXPERTS = 8
        TOP_K = 2
        RANK = 16
        LORA_ALPHA = 32
        SCALING = LORA_ALPHA / RANK
        bs, seq, d_in = x.shape
        T = bs * seq
        xf = x.reshape(T, d_in)
        base = xf @ W_base.T + b_base
        logits = xf @ W_router.T
        rw, sel = jax.lax.top_k(logits, TOP_K)
        rw = jax.nn.softmax(rw, axis=-1)
        onehot = jax.nn.one_hot(sel, NUM_EXPERTS, dtype=rw.dtype)
        w = jnp.einsum('tk,tke->te', rw, onehot)
        h = jnp.einsum('td,erd->ter', xf, A)
        lora = jnp.einsum('ter,te,eor->to', h, w, B) * SCALING
        return (base + lora).reshape(bs, seq, -1)

    def _L1_cond_ref(u, length, log_dt, C, log_A_real, A_imag, D):
        import math
        import jax, jax.numpy as jnp
        import numpy as np
        H, N, B, L = (32, 64, 16, 512)
        DT_MIN, DT_MAX = (0.001, 0.1)

        def _get_kernel(log_dt, C, log_A_real, A_imag, length):
            Cc = C[..., 0] + 1j * C[..., 1]
            dt = jnp.exp(log_dt)
            A = -jnp.exp(log_A_real) + 1j * A_imag
            dtA = A * dt[:, None]
            P = dtA[:, :, None] * jnp.arange(length, dtype=jnp.float32)
            Cs = Cc * (jnp.exp(dtA) - 1.0) / A
            K = 2.0 * jnp.einsum('hn,hnl->hl', Cs, jnp.exp(P)).real
            return K
        Bq, Hq, Lq = u.shape
        mask = (jnp.arange(Lq) < length[:, None]).astype(u.dtype)
        u_m = u * mask[:, None, :]
        kernel = _get_kernel(log_dt, C, log_A_real, A_imag, Lq)
        n = 2 * Lq
        k_f = jnp.fft.rfft(kernel, n=n)
        u_f = jnp.fft.rfft(u_m, n=n)
        y = jnp.fft.irfft(u_f * k_f, n=n)[..., :Lq]
        y = y + u_m * D[:, None]
        return y * mask[:, None, :]

    def _L1_ffn_ref(x, up, down, perm):
        import jax, jax.numpy as jnp
        import numpy as np
        B, L, H, Dh, M = (4, 256, 16, 32, 128)
        D = H * Dh
        b, l, Dm = x.shape
        h, d = (up.shape[0], up.shape[1])
        unperm = jnp.argsort(perm)
        t = x.reshape(b * l, Dm)
        t = t[:, perm]
        t = t.reshape(b * l, h, d)
        t = jnp.einsum('bhd,hdm->bhm', t, up)
        t = jax.nn.gelu(t, approximate=False)
        t = jnp.einsum('bhm,hmd->bhd', t, down)
        t = t.reshape(b * l, h * d)
        t = t[:, unperm]
        out = t.reshape(b, l, Dm)
        return out
    x = x + _L0_ffn_ref(_L0_cond_ref(x, itok_B_0_7, _lenS, itok_B_2182_4065, L0_cond_W_sess, L0_cond_b_sess, L0_cond_W2, L0_cond_b2), L0_ffn_W_base, L0_ffn_b_base, L0_ffn_W_router, L0_ffn_A, L0_ffn_B)
    x = x + _L1_ffn_ref(_L1_cond_ref(x, itok_B_8_3872, L1_cond_log_dt, L1_cond_C, L1_cond_log_A_real, L1_cond_A_imag, L1_cond_D), L1_ffn_up, L1_ffn_down, L1_ffn_perm)
    return x

_drawn_inputs = setup_inputs


def setup_inputs(seed=0):
    import zlib

    import numpy as np

    out = dict(_drawn_inputs(seed))
    spreads = {'L1_cond_log_A_real': (-0.6931471824645996, 0.2)}
    factors = {'L0_cond_b_sess': 2.978, 'L0_ffn_W_router': 6.667, 'L0_ffn_A': 4.08, 'L0_ffn_B': 4.627}
    for name, (base, spread) in spreads.items():
        noise = np.random.default_rng([zlib.crc32(name.encode()), seed]).standard_normal(out[name].shape)
        drawn = base * np.exp(spread * noise) if base else spread * noise
        out[name] = jnp.asarray(drawn.astype(out[name].dtype))
    for name, factor in factors.items():
        out[name] = (out[name] * factor).astype(out[name].dtype)
    return out
```

```python
from contextlib import ExitStack

import concourse.bass as bass
from concourse import mybir

P = 128
ALU = mybir.AluOpType
ACT = mybir.ActivationFunctionType
F32 = mybir.dt.float32
I32 = mybir.dt.int32
AX_X = mybir.AxisListType.X

ROUND = 1.5 * 2.0 ** 23
LOG2E = 1.4426950408889634
LN2_HI, LN2_LO = 0.693359375, -2.12194440e-4
EXP_COEFFS = [1 / 5040, 1 / 720, 1 / 120, 1 / 24, 1 / 6, 1 / 2, 1.0]
TWO_PI_PARTS = (6.28125, 1.9340515136718750e-3, 1.2556660176e-6)
HALF_PI = 1.5707963267948966
PI_BELOW = 3.1415925
BIG = 3.0e38


def adaln_ffn_kernel(nc, x, sess_id, sess_by4, seq_len, conv_len, chan_by4, w_sess, b_sess, w2, b2, w_base_t, b_base_c,
                     low_router_t, lora_b_t, log_dt, c_ri, log_a_re, a_im, d_skip, up, down, perm_c, out):
    B, C, T = x.shape
    NS, _, HID = w_sess.shape
    NE = low_router_t.shape[1] - P
    RANK = P // NE
    NST = a_im.shape[1]
    NH, DH, M = up.shape
    KC = T // P
    NT = B * C // T
    TOK = T
    BPG = P // C
    NG = B // BPG
    GPT = NG // NT
    BPT = B // NT
    PAIRS = BPT // 2
    LR = P + NE
    CPT = C // NT
    KLEN = T + P
    NI, NJ = 16, 32
    NL = NJ + 2 * NI
    TBUF = 8

    k_rev = nc.dram_tensor("k_rev", [C, KLEN], F32, kind="Internal")
    y_rows = [nc.dram_tensor(f"y_rows{g}", [T, TOK], F32, kind="Internal") for g in range(NT)]
    z_rows = [nc.dram_tensor(f"z_rows{g}", [T, TOK], F32, kind="Internal") for g in range(NT)]

    with ExitStack() as ctx:
        def sb(name, shape, dt=F32):
            return ctx.enter_context(nc.sbuf_tensor(name, shape, dt))

        def sem(name):
            return ctx.enter_context(nc.semaphore(name))

        ident = sb("ident", [P, P])
        p_int = sb("p_int", [P, 1], I32)
        chan_int = sb("chan_int", [P, 1], I32)
        par_int = sb("par_int", [P, 1], I32)
        chan_of_p = sb("chan_of_p", [P, 1])
        parity = sb("parity", [P, 2])
        p_col = sb("p_col", [P, 1])
        step_of = sb("step_of", [P, KC])
        rstep_of = sb("rstep_of", [P, KC])
        ramp = sb("ramp", [P, NE])
        sid_w = sb("sid_w", [P, NG], I32)
        len_w = sb("len_w", [P, NG], I32)
        row_w = sb("row_w", [P, NG], I32)
        cmask = sb("cmask", [P, NG])
        cmask2 = sb("cmask2", [P, NG, 2])
        w_raw = sb("w_raw", [P, NG, HID])
        w_bd = sb("w_bd", [P, NG, 2, HID])
        sid_e = sb("sid_e", [NS, B], I32)
        onehot_e = sb("onehot_e", [NS, 2, B // 2])
        bs_sb = sb("bs_sb", [NS, HID])
        bias_h = sb("bias_h", [P, B // 2])
        w2_bd = sb("w2_bd", [P, 2 * C])
        b2_row = sb("b2_row", [P, C])
        seq_sb = sb("seq_sb", [P, B], I32)
        tmask = sb("tmask", [P, KC, B])
        clen_sb = sb("clen_sb", [P, B], I32)
        lmask = sb("lmask", [P, KC, B])
        wb_t = sb("wb_t", [P, KC, T])
        ar_t = sb("ar_t", [P, KC, LR])
        b_t = sb("b_t", [P, T])
        bb_col = sb("bb_col", [P, KC])
        up_sb = sb("up_sb", [P, NH // 4, M])
        down_sb = sb("down_sb", [P, NH, DH])
        perm_sb = sb("perm_sb", [P, KC], I32)
        yrow_sb = sb("yrow_sb", [P, KC], I32)
        x_sb = sb("x_sb", [P, NG, T])
        hid0 = sb("hid0", [P, 4, T])
        c0 = sb("c0", [P, 2, KC, TOK])
        lg = sb("lg", [P, GPT, NE])
        rt = sb("rt", [P, 6, GPT, NE])
        rs = sb("rs", [P, 8, GPT])
        hw = sb("hw", [P, GPT, P])
        hw_t = sb("hw_t", [P, TOK])
        u = sb("u", [P, KC, C, B])
        kz = sb("kz", [C, NST + 1])
        kc = sb("kc", [C, NST, 2])
        kai = sb("kai", [C, NST])
        ke = sb("ke", [C, NST + 1])
        ks = sb("ks", [C, 16, NST + 1])
        ksc = sb("ksc", [C, NST + 1], I32)
        ksin = sb("ksin", [C, 2, NST])
        k4 = sb("k4", [C, 4, 2, NST])
        k4t = sb("k4t", [P, 4, C])
        lgrid = sb("lgrid", [P, NL])
        off_q = sb("off_q", [P, NL])
        off_r = sb("off_r", [P, NL])
        ph = sb("ph", [P, C, NL])
        turns = sb("turns", [P, C, NL])
        decay = sb("decay", [P, C, NJ + NI])
        fine = sb("fine", [P, C, NJ])
        coarse = sb("coarse", [P, C, NI])
        coarse2 = sb("coarse2", [P, C, NI])
        d_bc = sb("d_bc", [NI, C])
        last_p = sb("last_p", [NI, 1])
        k_sb = sb("k_sb", [NI, C, NJ])
        zeros = sb("zeros", [C, P])
        toep = sb("toep", [P, TBUF, T])
        yt = sb("yt", [P, KC, TOK])
        yp = x_sb[:, 0:2 * KC, :].rearrange("p (two k) n -> p two k n", two=2)
        hid1 = x_sb[:, 2 * KC:2 * KC + 4, :]
        ob = x_sb[:, 2 * KC + 4:NG, :]
        ot = hid0
        zn = c0

        bank = [ctx.enter_context(nc.psum_tensor(f"bank{i}", [P, 512], F32)) for i in range(8)]
        ps_h = bank[0:2]
        ps_c = bank[2:6]
        ps_f = bank[6:8]
        ps_y = bank[0:2]
        ps_u = bank[2:5]
        ps_o = bank[5:7]
        ps_z = bank[7]

        s_idx = sem("s_idx")
        s_seq = sem("s_seq")
        s_bs = sem("s_bs")
        s_w2 = sem("s_w2")
        s_x = [sem(f"s_x{i}") for i in range(NG)]
        s_wb = sem("s_wb")
        s_ar = sem("s_ar")
        s_bb = sem("s_bb")
        s_kin = sem("s_kin")
        s_l1 = sem("s_l1")
        s_dbc = sem("s_dbc")
        s_cst = sem("s_cst")
        s_idn = sem("s_idn")
        s_z0 = sem("s_z0")
        s_row = sem("s_row")
        s_wg = [sem(f"s_wg{i}") for i in range(NT)]
        s_wbd = sem("s_wbd")
        s_ohe = sem("s_ohe")
        s_yrow = sem("s_yrow")
        s_hd = sem("s_hd")
        s_hg = sem("s_hg")
        s_hu = sem("s_hu")
        s_cv = sem("s_cv")
        s_c0 = sem("s_c0")
        s_fd = [sem(f"s_fd{i}") for i in range(2)]
        s_ff = [sem(f"s_ff{i}") for i in range(2)]
        s_hw = sem("s_hw")
        s_hwt = sem("s_hwt")
        s_ex = sem("s_ex")
        s_exd = sem("s_exd")
        s_u = sem("s_u")
        s_ka = sem("s_ka")
        s_kb = sem("s_kb")
        s_k4 = sem("s_k4")
        s_kt = sem("s_kt")
        s_ks = sem("s_ks")
        s_kr = sem("s_kr")
        s_tp = [sem(f"s_tp{i}") for i in range(TBUF)]
        s_cd = sem("s_cd")
        s_ye = sem("s_ye")
        s_ys = [sem(f"s_ys{g}") for g in range(NT)]
        s_yg = [sem(f"s_yg{g}") for g in range(NT)]
        s_ud = sem("s_ud")
        s_ug = sem("s_ug")
        s_od = sem("s_od")
        s_oe = sem("s_oe")
        s_zs = [sem(f"s_zs{g}") for g in range(NT)]
        s_zl = [sem(f"s_zl{g}") for g in range(NT)]
        s_za = sem("s_za")
        s_zd = sem("s_zd")
        s_ze = sem("s_ze")
        s_out = [sem(f"s_out{i}") for i in range(4)]
        s_dch = sem("s_dch")

        names = ["bias", "k4"]
        for g in range(NT):
            names += [f"lr{g}0", f"lr{g}1", f"hw{g}"] + [f"oc{g}{i}" for i in range(KC)]
            if g == 0:
                names += ["k0", "k1"]
        unit = {n: i for i, n in enumerate(names)}

        def ring(n):
            return ps_f[unit[n] % 2]

        def wait_filled(eng, n):
            eng.wait_ge(s_fd[unit[n] % 2], unit[n] // 2 + 1)

        def wait_free(eng, n):
            if unit[n] >= 2:
                eng.wait_ge(s_ff[unit[n] % 2], unit[n] // 2)

        def filled(ins, n):
            ins.then_inc(s_fd[unit[n] % 2], 1)

        def freed(ins, n):
            ins.then_inc(s_ff[unit[n] % 2], 1)

        sess_even_odd = sess_id.rearrange("(one b) -> one b", one=1)

        block = ctx.enter_context(nc.Block())

        @block.sync
        def _(sp):
            for b4 in range(BPG):
                sp.dma_start(sid_w[C * b4:C * (b4 + 1), :], sess_by4[b4:b4 + 1, :].broadcast_to([C, NG])).then_inc(s_idx, 16)
                sp.dma_start(len_w[C * b4:C * (b4 + 1), :], chan_by4[b4:b4 + 1, :].broadcast_to([C, NG])).then_inc(s_idx, 16)
            sp.dma_start(sid_e[:, :], sess_even_odd.broadcast_to([NS, B])).then_inc(s_bs, 16)
            sp.dma_start(bs_sb[:, :], b_sess).then_inc(s_bs, 16)
            xg = x.rearrange("(g b) c t -> g (b c) t", b=BPG)
            for i in range(GPT):
                sp.dma_start(x_sb[:, i, :], xg[i]).then_inc(s_x[i], 16)
            sp.wait_ge(s_z0, 1)
            for i in range(2):
                sp.dma_start(w2_bd[HID * i:HID * (i + 1), C * i:C * (i + 1)], w2).then_inc(s_w2, 16)
            sp.dma_start(b2_row[:, :], b2.rearrange("(one s) -> one s", one=1).broadcast_to([P, C])).then_inc(s_w2, 16)
            sp.dma_start(seq_sb[:, :], seq_len.rearrange("(one b) -> one b", one=1).broadcast_to([P, B])).then_inc(s_seq, 16)
            sp.dma_start(clen_sb[:, :], conv_len.rearrange("(one b) -> one b", one=1).broadcast_to([P, B])).then_inc(s_seq, 16)
            sp.dma_start(ar_t[:, :, :], low_router_t.rearrange("(k p) n -> p k n", p=P)).then_inc(s_ar, 16)
            sp.dma_start(wb_t[:, :, :], w_base_t.rearrange("(k p) o -> p k o", p=P)).then_inc(s_wb, 16)
            sp.dma_start(b_t[:, :], lora_b_t).then_inc(s_wb, 16)
            sp.dma_start(bb_col[:, :], b_base_c).then_inc(s_bb, 16)
            for i in range(GPT, NG):
                sp.dma_start(x_sb[:, i, :], xg[i]).then_inc(s_x[i], 16)
            sp.dma_start(up_sb[:, :, :], up.rearrange("(q h) d m -> (h d) q m", h=4)).then_inc(s_l1, 16)
            sp.dma_start(down_sb[:, :, :], down.rearrange("h m d -> m h d")).then_inc(s_l1, 16)
            sp.dma_start(k_rev[:, T:KLEN], zeros[:, :]).then_inc(s_kr, 16)
            sp.wait_ge(s_ks, 1)
            sp.dma_start(k_rev[:, 0:T].rearrange("h (i j) -> i h j", j=NJ), k_sb[:, :, :]).then_inc(s_kr, 16)
            sp.wait_ge(s_kr, 32)

            def load_toeplitz(g):
                for h in range(CPT * g, CPT * (g + 1)):
                    if h >= TBUF:
                        sp.wait_ge(s_cd, h - TBUF + 1)
                    src = bass.AP(tensor=k_rev, offset=h * KLEN, ap=[[1, P], [1, T]])
                    sp.dma_start(toep[:, h % TBUF, :], src).then_inc(s_tp[h % TBUF], 16)

            def store_rows(g):
                sp.wait_ge(s_ye, (g + 1) * CPT // 2)
                sp.dma_start(y_rows[g][:, :].rearrange("(k p) n -> p k n", p=P), yt[:, :, :]).then_inc(s_ys[g], 16)

            def load_back(g):
                sp.wait_ge(s_zs[g], 16 * KC)
                if g >= 2:
                    sp.wait_ge(s_zd, 4 * (g - 1))
                sp.dma_start(zn[:, g % 2, :, :], z_rows[g][:, :].rearrange("(k p) n -> p k n", p=P)).then_inc(s_zl[g], 16)

            def store_out(g):
                for s in range(4):
                    sp.wait_ge(s_ze, 4 * g + s + 1)
                    for i in range(2):
                        sp.dma_start(out[:, CPT * g + 2 * s + i, :], ob[B * i:B * (i + 1), s, :]).then_inc(s_out[s], 16)

            load_toeplitz(0)
            store_rows(0)
            load_toeplitz(1)
            store_rows(1)
            load_toeplitz(2)
            load_back(0)
            store_rows(2)
            store_out(0)
            load_toeplitz(3)
            load_back(1)
            store_rows(3)
            store_out(1)
            load_back(2)
            load_back(3)
            store_out(2)
            store_out(3)
            for s in range(4):
                sp.wait_ge(s_out[s], 32 * NT)

        @block.gpsimd
        def _(pool):
            nc.gpsimd.memset(w2_bd[:, :], 0.0)
            nc.gpsimd.memset(zeros[:, :], 0.0).then_inc(s_z0, 1)
            nc.gpsimd.iota(p_int[:, :], [[0, 1]], base=0, channel_multiplier=1)
            nc.gpsimd.iota(p_col[:, :], [[0, 1]], base=0, channel_multiplier=1, allow_small_or_imprecise_dtypes=True)
            nc.gpsimd.iota(step_of[:, :], [[P, KC]], base=0, channel_multiplier=1, allow_small_or_imprecise_dtypes=True)
            nc.gpsimd.iota(rstep_of[:, :], [[P, KC]], base=P - 1, channel_multiplier=-1, allow_small_or_imprecise_dtypes=True)
            nc.gpsimd.iota(ramp[:, :], [[-1, NE]], base=NE, channel_multiplier=0, allow_small_or_imprecise_dtypes=True)
            nc.gpsimd.iota(lgrid[:, 0:NJ], [[-1, NJ]], base=NJ - 1, channel_multiplier=0, allow_small_or_imprecise_dtypes=True)
            nc.gpsimd.iota(lgrid[:, NJ:NL], [[0, 2], [-NJ, NI]], base=T - NJ, channel_multiplier=0,
                           allow_small_or_imprecise_dtypes=True).then_inc(s_cst, 1)
            nc.gpsimd.memset(ident[:, :], 0.0).then_inc(s_idn, 1)
            pool.wait_ge(s_idn, 1)
            nc.gpsimd.affine_select(out=ident[:, :], in_=ident[:, :], compare_op=ALU.not_equal, fill=1.0, base=0,
                                    pattern=[[-1, P]], channel_multiplier=1).then_inc(s_idn, 1)
            pool.wait_ge(s_row, 1)
            for i in range(NG):
                nc.gpsimd.indirect_dma_start(
                    out=w_raw[:, i, :], out_offset=None, in_=w_sess.rearrange("e c h -> (e c) h"),
                    in_offset=bass.IndirectOffsetOnAxis(ap=row_w[:, i:i + 1], axis=0)).then_inc(s_wg[i // GPT], 16)
            for g in range(NT):
                pool.wait_ge(s_cv, KC * (g + 1))
                for k in range(KC):
                    v = c0[:, g % 2, k, :].rearrange("p (b s) -> p b s", s=C)
                    m = tmask[:, k, BPT * g:BPT * (g + 1)].unsqueeze(2).broadcast_to([P, BPT, C])
                    nc.gpsimd.tensor_tensor(v, v, m, ALU.mult).then_inc(s_c0, 1)

            def gather(g):
                pool.wait_ge(s_ys[g], 16)
                if g >= 2:
                    pool.wait_ge(s_ud, NH * (g - 1))
                for q in range(KC):
                    nc.gpsimd.indirect_dma_start(
                        out=yp[:, g % 2, q, :], out_offset=None, in_=y_rows[g][:, :],
                        in_offset=bass.IndirectOffsetOnAxis(ap=yrow_sb[:, q:q + 1], axis=0)).then_inc(s_yg[g], 16)

            def scatter(g):
                for q in range(KC):
                    pool.wait_ge(s_oe, KC * g + q + 1)
                    nc.gpsimd.indirect_dma_start(
                        out=z_rows[g][:, :], out_offset=bass.IndirectOffsetOnAxis(ap=perm_sb[:, q:q + 1], axis=0),
                        in_=ot[:, q, :], in_offset=None).then_inc(s_zs[g], 16)

            pool.wait_ge(s_yrow, 1)
            gather(0)
            gather(1)
            scatter(0)
            gather(2)
            scatter(1)
            gather(3)
            scatter(2)
            scatter(3)

        @block.scalar
        def _(act):
            act.dma_start(kz[:, 0:NST], log_a_re).then_inc(s_kin, 16)
            act.dma_start(kz[:, NST:NST + 1], log_dt.rearrange("(h one) -> h one", one=1)).then_inc(s_kin, 16)
            act.dma_start(kai[:, :], a_im).then_inc(s_kin, 16)
            act.dma_start(kc[:, :, :], c_ri).then_inc(s_kin, 16)
            act.dma_start(perm_sb[:, :], perm_c).then_inc(s_l1, 16)
            act.dma_start(d_bc[:, :], d_skip.rearrange("(one h) -> one h", one=1).broadcast_to([NI, C])).then_inc(s_dbc, 16)
            act.wait_ge(s_ka, 1)
            nc.scalar.activation(ksin[:, 0, :], ks[:, 5, 0:NST], ACT.Sin)
            nc.scalar.activation(ksin[:, 1, :], ks[:, 5, 0:NST], ACT.Sin, scale=0.5).then_inc(s_kb, 1)

            def gelus(g):
                for j in range(PAIRS):
                    n = PAIRS * g + j
                    act.wait_ge(s_hd, n + 1)
                    if n >= 4:
                        act.wait_ge(s_hu, n - 3)
                    nc.scalar.activation(hid0[:, n % 4, :], ps_h[n % 2][:, :], ACT.Gelu,
                                         bias=bias_h[:, n:n + 1]).then_inc(s_hg, 1)

            act.wait_ge(s_ff[unit["bias"] % 2], 1)
            gelus(0)
            act.wait_ge(s_bb, 16)
            for g in range(NT):
                if g == 0:
                    act.wait_ge(s_ka, 2)
                    nc.scalar.activation(turns[:, :, :], ph[:, :, :], ACT.Sin)
                    nc.scalar.activation(decay[:, :, :], decay[:, :, :], ACT.Exp).then_inc(s_kb, 1)
                act.wait_ge(s_ex, g + 1)
                nc.scalar.activation(rs[:, 3, :], rs[:, 2, :], ACT.Exp).then_inc(s_exd, 1)
                if g + 1 < NT:
                    gelus(g + 1)
                wait_filled(act, f"hw{g}")
                ins = nc.scalar.copy(hw_t[:, :], ring(f"hw{g}")[:, :])
                freed(ins, f"hw{g}")
                for i in range(KC):
                    wait_filled(act, f"oc{g}{i}")
                    ins = nc.scalar.activation(
                        u[:, i, :, BPT * g:BPT * (g + 1)].rearrange("p s b -> p b s"),
                        ring(f"oc{g}{i}")[:, :].rearrange("p (b s) -> p b s", s=C), ACT.Identity, bias=bb_col[:, i:i + 1])
                    freed(ins, f"oc{g}{i}")
            for n in range(NT * NH):
                act.wait_ge(s_ud, n + 1)
                if n >= 4:
                    act.wait_ge(s_od, n - 3)
                nc.scalar.activation(hid1[:, n % 4, :], ps_u[n % 3][:, :], ACT.Gelu).then_inc(s_ug, 1)

        @block.vector
        def _(dve):
            V = nc.vector
            chain = [0]

            def link(ins):
                chain[0] += 1
                ins.then_inc(s_dch, 1)
                dve.wait_ge(s_dch, chain[0])

            dve.wait_ge(s_cst, 1)
            link(V.tensor_scalar(chan_int[:, :], p_int[:, :], C - 1, None, ALU.bitwise_and))
            link(V.tensor_scalar(par_int[:, :], p_int[:, :], 5, 1, ALU.logical_shift_right, ALU.bitwise_and))
            link(V.tensor_copy(chan_of_p[:, :], chan_int[:, :]))
            link(V.tensor_copy(parity[:, 1:2], par_int[:, :]))
            dve.wait_ge(s_idx, 32 * BPG)
            V.tensor_scalar(row_w[:, :], sid_w[:, :], float(C), chan_of_p[:, 0:1], ALU.mult, ALU.add).then_inc(s_row, 1)
            link(V.tensor_scalar(parity[:, 0:1], parity[:, 1:2], -1.0, 1.0, ALU.mult, ALU.add))
            link(V.tensor_scalar(cmask[:, :], len_w[:, :], chan_of_p[:, 0:1], None, ALU.is_gt))
            link(V.tensor_tensor(cmask2[:, :, :], cmask[:, :].unsqueeze(2).broadcast_to([P, NG, 2]),
                                 parity[:, :].unsqueeze(1).broadcast_to([P, NG, 2]), ALU.mult))
            dve.wait_ge(s_bs, 32)
            V.tensor_scalar(onehot_e[:, :, :], sid_e[:, :].rearrange("e (b two) -> e two b", two=2), p_col[0:NS, 0:1], None,
                            ALU.is_equal).then_inc(s_ohe, 1)

            def exp_small(dst_p, dst_scale, z, n):
                link(V.tensor_scalar(ks[:, 0, 0:n], z, LOG2E, ROUND, ALU.mult, ALU.add))
                link(V.tensor_scalar(ks[:, 0, 0:n], ks[:, 0, 0:n], ROUND, -126.0, ALU.subtract, ALU.max))
                link(V.scalar_tensor_tensor(ks[:, 1, 0:n], ks[:, 0, 0:n], -LN2_HI, z, ALU.mult, ALU.add))
                link(V.scalar_tensor_tensor(ks[:, 1, 0:n], ks[:, 0, 0:n], -LN2_LO, ks[:, 1, 0:n], ALU.mult, ALU.add))
                link(V.tensor_scalar(dst_p, ks[:, 1, 0:n], EXP_COEFFS[0], None, ALU.mult))
                for c in EXP_COEFFS[1:]:
                    link(V.scalar_tensor_tensor(dst_p, dst_p, c, ks[:, 1, 0:n], ALU.add, ALU.mult))
                link(V.tensor_scalar(dst_scale, ks[:, 0, 0:n], 127.0, 2.0 ** 23, ALU.add, ALU.mult))

            dve.wait_ge(s_kin, 64)
            N1 = NST + 1
            exp_small(ks[:, 2, 0:N1], ksc[:, 0:N1], kz[:, :], N1)
            link(V.scalar_tensor_tensor(ke[:, :], ks[:, 2, 0:N1], 1.0, ksc[:, 0:N1].bitcast(F32), ALU.add, ALU.mult))
            dt = ke[:, NST:N1]
            re, im = k4[:, 0, 0, :], k4[:, 1, 0, :]
            link(V.tensor_scalar(re, ke[:, 0:NST], dt, -1.0, ALU.mult, ALU.mult))
            link(V.tensor_scalar(im, kai[:, :], dt, None, ALU.mult))
            link(V.tensor_scalar(ks[:, 4, 0:NST], im, 1.0 / (4 * HALF_PI), ROUND, ALU.mult, ALU.add))
            link(V.tensor_scalar(ks[:, 4, 0:NST], ks[:, 4, 0:NST], ROUND, None, ALU.subtract))
            src = im
            for part in TWO_PI_PARTS:
                link(V.scalar_tensor_tensor(ks[:, 5, 0:NST], ks[:, 4, 0:NST], -part, src, ALU.mult, ALU.add))
                src = ks[:, 5, 0:NST]
            V.tensor_scalar(ks[:, 5, 0:NST], src, -PI_BELOW, PI_BELOW, ALU.max, ALU.min).then_inc(s_ka, 1)
            exp_small(ks[:, 2, 0:NST], ksc[:, 0:NST], re, NST)
            scale = ksc[:, 0:NST].bitcast(F32)
            em1, ex = ks[:, 6, 0:NST], ks[:, 7, 0:NST]
            link(V.tensor_scalar(ks[:, 3, 0:NST], scale, 1.0, None, ALU.subtract))
            link(V.tensor_tensor(em1, ks[:, 2, 0:NST], scale, ALU.mult))
            link(V.tensor_tensor(em1, em1, ks[:, 3, 0:NST], ALU.add))
            link(V.tensor_scalar(ex, em1, 1.0, None, ALU.add))
            dve.wait_ge(s_kb, 1)
            er, ei = ks[:, 8, 0:NST], ks[:, 9, 0:NST]
            link(V.tensor_tensor(ei, ex, ksin[:, 0, :], ALU.mult))
            link(V.tensor_tensor(er, ksin[:, 1, :], ksin[:, 1, :], ALU.mult))
            link(V.tensor_tensor(er, er, ex, ALU.mult))
            link(V.scalar_tensor_tensor(er, er, -2.0, em1, ALU.mult, ALU.add))
            cr, ci = kc[:, :, 0], kc[:, :, 1]
            nr, ni, t1 = ks[:, 10, 0:NST], ks[:, 11, 0:NST], ks[:, 12, 0:NST]
            link(V.tensor_tensor(nr, cr, er, ALU.mult))
            link(V.tensor_tensor(t1, ci, ei, ALU.mult))
            link(V.tensor_tensor(nr, nr, t1, ALU.subtract))
            link(V.tensor_tensor(ni, cr, ei, ALU.mult))
            link(V.tensor_tensor(t1, ci, er, ALU.mult))
            link(V.tensor_tensor(ni, ni, t1, ALU.add))
            ar, ai, inv = ks[:, 13, 0:NST], kai[:, :], ks[:, 14, 0:NST]
            link(V.tensor_scalar(ar, ke[:, 0:NST], -1.0, None, ALU.mult))
            link(V.tensor_tensor(inv, ar, ar, ALU.mult))
            link(V.tensor_tensor(t1, ai, ai, ALU.mult))
            link(V.tensor_tensor(inv, inv, t1, ALU.add))
            link(V.reciprocal(inv, inv))
            link(V.tensor_tensor(t1, nr, ar, ALU.mult))
            link(V.tensor_tensor(er, ni, ai, ALU.mult))
            link(V.tensor_tensor(t1, t1, er, ALU.add))
            link(V.tensor_tensor(ei, ni, ar, ALU.mult))
            link(V.tensor_tensor(er, nr, ai, ALU.mult))
            link(V.tensor_tensor(ei, ei, er, ALU.subtract))
            link(V.scalar_tensor_tensor(k4[:, 2, 0, :], t1, 2.0, inv, ALU.mult, ALU.mult))
            link(V.scalar_tensor_tensor(k4[:, 2, 1, :], ei, -2.0, inv, ALU.mult, ALU.mult))
            V.tensor_copy(k4[:, 0, 1, :], re)
            V.tensor_copy(k4[:, 1, 1, :], im)
            V.tensor_copy(k4[:, 3, 0, :], k4[:, 2, 1, :])
            V.tensor_scalar(k4[:, 3, 1, :], k4[:, 2, 0, :], -1.0, None, ALU.mult).then_inc(s_k4, 1)

            def weights(g):
                dve.wait_ge(s_wg[g], 16 * GPT)
                for i in range(2):
                    sl = slice(GPT * g, GPT * (g + 1))
                    last = V.tensor_tensor(w_bd[:, sl, i, :], w_raw[:, sl, :],
                                           cmask2[:, sl, i].unsqueeze(2).broadcast_to([P, GPT, HID]), ALU.mult)
                last.then_inc(s_wbd, 1)

            weights(0)
            wait_filled(dve, "bias")
            ins = V.tensor_copy(bias_h[:, :], ring("bias")[:, 0:B // 2])
            freed(ins, "bias")
            dve.wait_ge(s_seq, 32)
            V.tensor_tensor(tmask[:, :, :], step_of[:, :].unsqueeze(2).broadcast_to([P, KC, B]),
                            seq_sb[:, :].unsqueeze(1).broadcast_to([P, KC, B]), ALU.is_lt)
            V.tensor_tensor(lmask[:, :, :], rstep_of[:, :].unsqueeze(2).broadcast_to([P, KC, B]),
                            clen_sb[:, :].unsqueeze(1).broadcast_to([P, KC, B]), ALU.is_lt)

            def cond_out(g):
                if g == 0:
                    dve.wait_ge(s_w2, 48)
                dve.wait_ge(s_hu, PAIRS * (g + 1))
                if g >= 2:
                    wait_filled(dve, f"oc{g - 2}{KC - 1}")
                for k in range(KC):
                    V.tensor_tensor(c0[:, g % 2, k, :].rearrange("p (b s) -> p b s", s=C),
                                    ps_c[k][:, :].rearrange("p (b s) -> p b s", s=C),
                                    b2_row[:, :].unsqueeze(1).broadcast_to([P, BPT, C]), ALU.add).then_inc(s_cv, 1)

            def route(g):
                for i in range(2):
                    wait_filled(dve, f"lr{g}{i}")
                    link(V.tensor_copy(lg[:, 2 * i:2 * i + 2, :],
                                       ring(f"lr{g}{i}")[:, 0:2 * LR].rearrange("p (s n) -> p s n", n=LR)[:, :, P:LR]))

                def wide(a):
                    return a.unsqueeze(2).broadcast_to([P, GPT, NE])

                ramps = ramp[:, :].unsqueeze(1).broadcast_to([P, GPT, NE])

                def top(logits, m, first, hot):
                    link(V.tensor_reduce(rs[:, m, :], logits, AX_X, ALU.max))
                    link(V.tensor_tensor(rt[:, 0], logits, wide(rs[:, m, :]), ALU.is_equal))
                    link(V.tensor_tensor(rt[:, 0], rt[:, 0], ramps, ALU.mult))
                    link(V.tensor_reduce(rs[:, first, :], rt[:, 0], AX_X, ALU.max))
                    link(V.tensor_tensor(rt[:, hot], ramps, wide(rs[:, first, :]), ALU.is_equal))

                top(lg[:, :, :], 0, 4, 1)
                link(V.scalar_tensor_tensor(rt[:, 2], rt[:, 1], -BIG, lg[:, :, :], ALU.mult, ALU.add))
                top(rt[:, 2], 1, 5, 3)
                V.tensor_tensor(rs[:, 2, :], rs[:, 1, :], rs[:, 0, :], ALU.subtract).then_inc(s_ex, 1)
                dve.wait_ge(s_exd, g + 1)
                link(V.tensor_scalar(rs[:, 6, :], rs[:, 3, :], 1.0, None, ALU.add))
                link(V.reciprocal(rs[:, 6, :], rs[:, 6, :]))
                link(V.tensor_scalar(rs[:, 6, :], rs[:, 6, :], 2.0, None, ALU.mult))
                link(V.tensor_tensor(rs[:, 7, :], rs[:, 6, :], rs[:, 3, :], ALU.mult))
                link(V.tensor_tensor(rt[:, 1], rt[:, 1], wide(rs[:, 6, :]), ALU.mult))
                link(V.tensor_tensor(rt[:, 3], rt[:, 3], wide(rs[:, 7, :]), ALU.mult))
                link(V.tensor_tensor(rt[:, 4], rt[:, 1], rt[:, 3], ALU.add))
                if g >= 1:
                    wait_filled(dve, f"hw{g - 1}")
                for i in range(2):
                    ins = V.tensor_tensor(
                        hw[:, 2 * i:2 * i + 2, :].rearrange("p s (e r) -> p s e r", e=NE),
                        ring(f"lr{g}{i}")[:, 0:2 * LR].rearrange("p (s n) -> p s n", n=LR)[:, :, 0:P].rearrange("p s (e r) -> p s e r", e=NE),
                        rt[:, 4, 2 * i:2 * i + 2, :].unsqueeze(3).broadcast_to([P, 2, NE, RANK]), ALU.mult)
                    freed(ins, f"lr{g}{i}")

            def kernel_tables():
                wait_filled(dve, "k4")
                ins = V.tensor_copy(k4t[:, :, :], ring("k4")[:, 0:4 * C].rearrange("p (a h) -> p a h", a=4))
                freed(ins, "k4")
                dve.wait_ge(s_ff[unit["k4"] % 2], unit["k4"] // 2 + 1)
                for t, v in ((off_q, 0.25), (off_r, HALF_PI)):
                    V.tensor_scalar(t[:, 0:NJ], p_col[:, :].broadcast_to([P, NJ]), P / 2.0, v, ALU.is_lt, ALU.mult)
                    V.memset(t[:, NJ:NJ + NI], 0.0)
                    link(V.memset(t[:, NJ + NI:NL], v))
                lb = lgrid[:, :].unsqueeze(1).broadcast_to([P, C, NL])
                V.tensor_tensor(decay[:, :, :], k4t[:, 0, :].unsqueeze(2).broadcast_to([P, C, NJ + NI]),
                                lgrid[:, 0:NJ + NI].unsqueeze(1).broadcast_to([P, C, NJ + NI]), ALU.mult)
                link(V.tensor_tensor(ph[:, :, :], k4t[:, 1, :].unsqueeze(2).broadcast_to([P, C, NL]), lb, ALU.mult))
                link(V.scalar_tensor_tensor(turns[:, :, :], ph[:, :, :], 1.0 / (4 * HALF_PI),
                                            off_q[:, :].unsqueeze(1).broadcast_to([P, C, NL]), ALU.mult, ALU.add))
                link(V.tensor_scalar(turns[:, :, :], turns[:, :, :], ROUND, None, ALU.add))
                link(V.tensor_scalar(turns[:, :, :], turns[:, :, :], ROUND, None, ALU.subtract))
                for part in TWO_PI_PARTS:
                    link(V.scalar_tensor_tensor(ph[:, :, :], turns[:, :, :], -part, ph[:, :, :], ALU.mult, ALU.add))
                link(V.tensor_tensor(ph[:, :, :], ph[:, :, :], off_r[:, :].unsqueeze(1).broadcast_to([P, C, NL]), ALU.add))
                V.tensor_scalar(ph[:, :, :], ph[:, :, :], -PI_BELOW, PI_BELOW, ALU.max, ALU.min).then_inc(s_ka, 1)

            def kernel_factors():
                dve.wait_ge(s_kb, 2)
                sines = turns
                link(V.tensor_tensor(coarse[:, :, :], sines[:, :, NJ + NI:NL],
                                     k4t[:, 2, :].unsqueeze(2).broadcast_to([P, C, NI]), ALU.mult))
                link(V.tensor_tensor(coarse2[:, :, :], sines[:, :, NJ:NJ + NI],
                                     k4t[:, 3, :].unsqueeze(2).broadcast_to([P, C, NI]), ALU.mult))
                link(V.tensor_tensor(coarse[:, :, :], coarse[:, :, :], coarse2[:, :, :], ALU.add))
                link(V.tensor_tensor(coarse[:, :, :], coarse[:, :, :], decay[:, :, NJ:NJ + NI], ALU.mult))
                V.tensor_tensor(fine[:, :, :], sines[:, :, 0:NJ], decay[:, :, 0:NJ], ALU.mult).then_inc(s_kt, 1)

            def kernel_out():
                dve.wait_ge(s_dbc, 16)
                link(V.tensor_scalar(last_p[:, :], p_col[0:NI, :], float(NI - 1), None, ALU.is_equal))
                link(V.tensor_scalar(d_bc[:, :], d_bc[:, :], last_p[:, 0:1], None, ALU.mult))
                HALF = C // 2
                for i in range(2):
                    wait_filled(dve, f"k{i}")
                    ins = V.tensor_copy(k_sb[:, HALF * i:HALF * (i + 1), :],
                                        ring(f"k{i}")[0:NI, :].rearrange("p (h j) -> p h j", j=NJ))
                    freed(ins, f"k{i}")
                    dve.wait_ge(s_ff[unit[f"k{i}"] % 2], unit[f"k{i}"] // 2 + 1)
                V.tensor_tensor(k_sb[:, :, NJ - 1], k_sb[:, :, NJ - 1], d_bc[:, :], ALU.add).then_inc(s_ks, 1)

            cond_out(0)
            kernel_tables()
            dve.wait_ge(s_l1, 48)
            V.tensor_scalar(yrow_sb[:, :], perm_sb[:, :], P - 1, None, ALU.bitwise_xor).then_inc(s_yrow, 1)
            for g in range(NT):
                route(g)
                if g + 1 < NT:
                    weights(g + 1)
                    cond_out(g + 1)
                if g == 0:
                    kernel_factors()
                    kernel_out()

            def conv_out(g):
                if g >= 1:
                    dve.wait_ge(s_ys[g - 1], 16)
                for j in range(CPT // 2):
                    n = CPT // 2 * g + j
                    dve.wait_ge(s_cd, 2 * (n + 1))
                    for i in range(2):
                        last = V.tensor_tensor(
                            yt[:, :, B * (2 * j + i):B * (2 * j + i + 1)],
                            ps_y[n % 2][:, KC * B * i:KC * B * (i + 1)].rearrange("p (k b) -> p k b", k=KC),
                            lmask[:, :, :], ALU.mult)
                    last.then_inc(s_ye, 1)

            def heads_out(g):
                for q in range(KC):
                    n = KC * g + q
                    dve.wait_ge(s_od, 4 * (n + 1))
                    if g >= 1 and q == 0:
                        dve.wait_ge(s_zs[g - 1], 16 * KC)
                    V.tensor_copy(ot[:, q, :], ps_o[n % 2][:, :]).then_inc(s_oe, 1)

            def residual(g):
                dve.wait_ge(s_zl[g], 16)
                for k in range(KC):
                    z = zn[:, g % 2, k, :].rearrange("p (h b) -> p h b", b=B)
                    V.tensor_tensor(z, z, u[:, k, CPT * g:CPT * (g + 1), :], ALU.add).then_inc(s_za, 1)

            def tokens_out(g):
                for s in range(4):
                    dve.wait_ge(s_zd, 4 * g + s + 1)
                    if g >= 1:
                        dve.wait_ge(s_out[s], 32 * g)
                    V.tensor_copy(ob[:, s, :], ps_z[:, :]).then_inc(s_ze, 1)

            conv_out(0)
            conv_out(1)
            heads_out(0)
            conv_out(2)
            residual(0)
            tokens_out(0)
            heads_out(1)
            conv_out(3)
            residual(1)
            tokens_out(1)
            heads_out(2)
            heads_out(3)
            residual(2)
            tokens_out(2)
            residual(3)
            tokens_out(3)

        @block.tensor
        def _(pe):
            mm = nc.tensor.matmul

            def cond(g):
                pe.wait_ge(s_wbd, g + 1)
                if g >= 1:
                    pe.wait_ge(s_cv, KC * g)

                def first(j):
                    n = PAIRS * g + j
                    grp, half = n // 2, n % 2
                    if half == 0:
                        pe.wait_ge(s_x[grp], 16)
                    if n >= 2:
                        pe.wait_ge(s_hg, n - 1)
                    mm(ps_h[n % 2][:, :], w_bd[64 * half:64 * (half + 1), grp, :, :], x_sb[64 * half:64 * (half + 1), grp, :],
                       start=True, stop=True).then_inc(s_hd, 1)

                first(0)
                for j in range(PAIRS):
                    n = PAIRS * g + j
                    if j + 1 < PAIRS:
                        first(j + 1)
                    pe.wait_ge(s_hg, n + 1)
                    for k in range(KC):
                        last = mm(ps_c[k][:, 64 * j:64 * (j + 1)], hid0[:, n % 4, P * k:P * (k + 1)], w2_bd[:, :],
                                  start=True, stop=True)
                    last.then_inc(s_hu, 1)

            pe.wait_ge(s_ohe, 1)
            for i in range(2):
                last = mm(ring("bias")[HID * i:HID * (i + 1), 0:B // 2], bs_sb[:, :], onehot_e[:, i, :], start=True, stop=True)
            filled(last, "bias")
            pe.wait_ge(s_w2, 48)
            cond(0)
            pe.wait_ge(s_idn, 2)
            pe.wait_ge(s_k4, 1)
            wait_free(pe, "k4")
            for a in range(4):
                last = nc.tensor.transpose(ring("k4")[:, C * a:C * (a + 1)], k4[:, a, :, :].rearrange("h c n -> h (c n)"),
                                           ident[0:C, 0:C])
            filled(last, "k4")

            pe.wait_ge(s_ar, 16)
            for g in range(NT):
                pe.wait_ge(s_c0, KC * (g + 1))
                for i in range(2):
                    wait_free(pe, f"lr{g}{i}")
                    for s in range(2):
                        for k in range(KC):
                            last = mm(ring(f"lr{g}{i}")[:, LR * s:LR * (s + 1)],
                                      c0[:, g % 2, k, P * (2 * i + s):P * (2 * i + s + 1)], ar_t[:, k, :],
                                      start=(k == 0), stop=(k == KC - 1))
                    filled(last, f"lr{g}{i}")
                if g + 1 < NT:
                    cond(g + 1)
                wait_free(pe, f"hw{g}")
                pe.wait_ge(s_ff[unit[f"lr{g}1"] % 2], unit[f"lr{g}1"] // 2 + 1)
                for s in range(GPT):
                    last = nc.tensor.transpose(ring(f"hw{g}")[:, P * s:P * (s + 1)], hw[:, s, :], ident[:, :])
                filled(last, f"hw{g}")
                if g == 0:
                    pe.wait_ge(s_wb, 32)
                for i in range(KC):
                    acc = ring(f"oc{g}{i}")
                    wait_free(pe, f"oc{g}{i}")
                    for s in range(GPT):
                        mm(acc[:, P * s:P * (s + 1)], x_sb[:, GPT * g + s, P * i:P * (i + 1)], ident[:, :],
                           start=(s == 0), stop=False, is_transpose=True, skip_group_check=True)
                    for k in range(KC):
                        mm(acc[:, :], wb_t[:, k, P * i:P * (i + 1)], c0[:, g % 2, k, :], start=False, stop=False,
                           skip_group_check=True)
                    if i == 0:
                        pe.wait_ge(s_ff[unit[f"hw{g}"] % 2], unit[f"hw{g}"] // 2 + 1)
                    last = mm(acc[:, :], b_t[:, P * i:P * (i + 1)], hw_t[:, :], start=False, stop=True, skip_group_check=True)
                    filled(last, f"oc{g}{i}")
                if g == 0:
                    pe.wait_ge(s_kt, 1)
                    for i in range(2):
                        wait_free(pe, f"k{i}")
                        for h in range(C // 2):
                            hh = C // 2 * i + h
                            last = mm(ring(f"k{i}")[0:NI, NJ * h:NJ * (h + 1)], coarse[:, hh, :], fine[:, hh, :],
                                      start=True, stop=True)
                        filled(last, f"k{i}")

            def conv(g):
                for c in range(CPT):
                    h = CPT * g + c
                    pe.wait_ge(s_tp[h % TBUF], 16 * (h // TBUF + 1))
                    if h % 2 == 0 and h >= 4:
                        pe.wait_ge(s_ye, h // 2 - 1)
                    acc = ps_y[(h // 2) % 2][:, KC * B * (h % 2):KC * B * (h % 2 + 1)]
                    for d in range(KC):
                        last = mm(acc[:, B * d:KC * B], toep[:, h % TBUF, P * (KC - 1 - d):P * (KC - d)],
                                  u[:, 0:KC - d, h, :], start=(d == 0), stop=(d == KC - 1), skip_group_check=True)
                    last.then_inc(s_cd, 1)

            def heads(g):
                pe.wait_ge(s_yg[g], 16 * KC)

                def rise(j):
                    n = NH * g + j
                    q, i = j // 4, j % 4
                    if n >= 3:
                        pe.wait_ge(s_ug, n - 2)
                    mm(ps_u[n % 3][:, :], up_sb[DH * i:DH * (i + 1), q, :], yp[DH * i:DH * (i + 1), g % 2, q, :],
                       start=True, stop=True).then_inc(s_ud, 1)

                rise(0)
                rise(1)
                for j in range(NH):
                    n = NH * g + j
                    q, i = j // 4, j % 4
                    if j + 2 < NH:
                        rise(j + 2)
                    pe.wait_ge(s_ug, n + 1)
                    if i == 0 and KC * g + q >= 2:
                        pe.wait_ge(s_oe, KC * g + q - 1)
                    mm(ps_o[(KC * g + q) % 2][DH * i:DH * (i + 1), :], down_sb[:, j, :], hid1[:, n % 4, :],
                       start=True, stop=True).then_inc(s_od, 1)

            def back(g):
                pe.wait_ge(s_za, KC * (g + 1))
                for s in range(4):
                    if 4 * g + s >= 1:
                        pe.wait_ge(s_ze, 4 * g + s)
                    for k in range(KC):
                        last = nc.tensor.transpose(ps_z[:, P * k:P * (k + 1)], zn[:, g % 2, k, P * s:P * (s + 1)], ident[:, :])
                    last.then_inc(s_zd, 1)

            for b in range(2):
                n = max(unit[f"oc{NT - 1}{i}"] for i in range(KC) if unit[f"oc{NT - 1}{i}"] % 2 == b)
                pe.wait_ge(s_ff[b], n // 2 + 1)
            pe.wait_ge(s_l1, 48)
            conv(0)
            conv(1)
            heads(0)
            conv(2)
            back(0)
            heads(1)
            conv(3)
            back(1)
            heads(2)
            heads(3)
            back(2)
            back(3)


def kernel(**inputs):
    import numpy as _np
    import concourse.bacc as _bacc
    from concourse import mybir as _mybir
    from concourse.bass_utils import run_bass_kernel_spmd as _run

    v = {name: _np.asarray(a) for name, a in inputs.items()}
    low = v["L0_ffn_A"].reshape(-1, v["L0_ffn_A"].shape[2])
    laid_out = {
        "x": v["x"],
        "sess_id": v["itok_B_0_7"],
        "sess_by4": v["itok_B_0_7"].reshape(-1, 4).T,
        "seq_len": v["itok_B_2182_4065"],
        "conv_len": v["itok_B_8_3872"],
        "chan_by4": v["_lenS"].reshape(-1, 4).T,
        "w_sess": v["L0_cond_W_sess"],
        "b_sess": v["L0_cond_b_sess"],
        "w2": v["L0_cond_W2"],
        "b2": v["L0_cond_b2"],
        "w_base_t": v["L0_ffn_W_base"].T,
        "b_base_c": v["L0_ffn_b_base"].reshape(-1, 128).T,
        "low_router_t": _np.concatenate([low, v["L0_ffn_W_router"]]).T,
        "lora_b_t": v["L0_ffn_B"].transpose(0, 2, 1).reshape(low.shape[0], -1),
        "log_dt": v["L1_cond_log_dt"],
        "c_ri": v["L1_cond_C"],
        "log_a_re": v["L1_cond_log_A_real"],
        "a_im": v["L1_cond_A_imag"],
        "d_skip": v["L1_cond_D"],
        "up": v["L1_ffn_up"],
        "down": v["L1_ffn_down"],
        "perm_c": v["L1_ffn_perm"].reshape(-1, 128).T,
    }
    nc = _bacc.Bacc("TRN2", target_bir_lowering=False, num_devices=1)
    arrays, args = {}, []
    for name, a in laid_out.items():
        a = _np.ascontiguousarray(a)
        arrays[f"in_{name}"] = a
        args.append(nc.dram_tensor(f"in_{name}", a.shape, _mybir.dt.from_np(a.dtype), kind="ExternalInput").ap())
    res = nc.dram_tensor("out_dram", v["x"].shape, _mybir.dt.float32, kind="ExternalOutput").ap()
    adaln_ffn_kernel(nc, *args, res)
    r = _run(nc, [arrays], core_ids=[0])
    return r.results[0]["out_dram"]
```

```python
from contextlib import ExitStack

import concourse.bass as bass
from concourse import mybir

P = 128
ALU = mybir.AluOpType
ACT = mybir.ActivationFunctionType
F32 = mybir.dt.float32
I32 = mybir.dt.int32
AX_X = mybir.AxisListType.X

ROUND = 1.5 * 2.0 ** 23
LOG2E = 1.4426950408889634
LN2_HI, LN2_LO = 0.693359375, -2.12194440e-4
EXP_COEFFS = [1 / 5040, 1 / 720, 1 / 120, 1 / 24, 1 / 6, 1 / 2, 1.0]
TWO_PI_PARTS = (6.28125, 1.9340515136718750e-3, 1.2556660176e-6)
HALF_PI = 1.5707963267948966
PI_BELOW = 3.1415925
BIG = 3.0e38


def adaln_ffn_kernel(nc, x, sess_id, sess_chan_by4, seq_len, conv_len, w_sess, b_sess, w2, b2, w_base_t, b_base_c,
                     low_router_t, lora_b_t, log_dt, c_ri, log_a_re, a_im, d_skip, up, down, perm_c, out):
    B, C, T = x.shape
    NS, _, HID = w_sess.shape
    NE = low_router_t.shape[1] - P
    RANK = P // NE
    NST = a_im.shape[1]
    NH, DH, M = up.shape
    KC = T // P
    NT = B * C // T
    TOK = T
    BPG = P // C
    NG = B // BPG
    GPT = NG // NT
    BPT = B // NT
    PAIRS = BPT // 2
    LR = P + NE
    CPT = C // NT
    KLEN = T + P
    NI, NJ = 16, 32
    NL = NJ + 2 * NI
    TBUF = 8

    k_rev = nc.dram_tensor("k_rev", [C, KLEN], F32, kind="Internal")
    y_rows = [nc.dram_tensor(f"y_rows{g}", [T, TOK], F32, kind="Internal") for g in range(NT)]
    out_rows = out.rearrange("g t h b -> (g t) (h b)")

    with ExitStack() as ctx:
        def sb(name, shape, dt=F32):
            return ctx.enter_context(nc.sbuf_tensor(name, shape, dt))

        def sem(name):
            return ctx.enter_context(nc.semaphore(name))

        ident = sb("ident", [P, P])
        p_int = sb("p_int", [P, 1], I32)
        chan_int = sb("chan_int", [P, 1], I32)
        par_int = sb("par_int", [P, 1], I32)
        chan_of_p = sb("chan_of_p", [P, 1])
        parity = sb("parity", [P, 2])
        p_col = sb("p_col", [P, 1])
        step_of = sb("step_of", [P, KC])
        rstep_of = sb("rstep_of", [P, KC])
        ramp = sb("ramp", [P, NE])
        sc_w = sb("sc_w", [P, 2 * NG], I32)
        row_w = sb("row_w", [P, NG], I32)
        cmask = sb("cmask", [P, NG])
        cmask2 = sb("cmask2", [P, NG, 2])
        w_raw = sb("w_raw", [P, NG, HID])
        w_bd = sb("w_bd", [P, NG, 2, HID])
        sid_e = sb("sid_e", [NS, B], I32)
        onehot_e = sb("onehot_e", [NS, 2, B // 2])
        bs_sb = sb("bs_sb", [NS, HID])
        bias_h = sb("bias_h", [P, B // 2])
        w2_bd = sb("w2_bd", [P, 2 * C])
        b2_row = sb("b2_row", [P, C])
        seq_sb = sb("seq_sb", [P, B], I32)
        tmask = sb("tmask", [P, KC, B])
        clen_sb = sb("clen_sb", [P, B], I32)
        lmask = sb("lmask", [P, KC, B])
        wb_t = sb("wb_t", [P, KC, T])
        ar_t = sb("ar_t", [P, KC, LR])
        b_t = sb("b_t", [P, T])
        bb_col = sb("bb_col", [P, KC])
        up_sb = sb("up_sb", [P, NH // 4, M])
        down_sb = sb("down_sb", [P, NH, DH])
        perm_sb = sb("perm_sb", [P, KC], I32)
        yrow_sb = sb("yrow_sb", [P, KC], I32)
        orow_sb = sb("orow_sb", [P, NT, KC], I32)
        x_sb = sb("x_sb", [P, NG, T])
        hid0 = sb("hid0", [P, 4, T])
        c0 = sb("c0", [P, 2, KC, TOK])
        lg = sb("lg", [P, GPT, NE])
        rt = sb("rt", [P, 6, GPT, NE])
        rs = sb("rs", [P, 8, GPT])
        re_ = sb("re_", [P, 5, GPT])
        re_i = sb("re_i", [P, GPT], I32)
        hw = sb("hw", [P, GPT, P])
        hw_t = sb("hw_t", [P, TOK])
        u = sb("u", [P, KC, C, B])
        kz = sb("kz", [C, NST + 1])
        kc = sb("kc", [C, NST, 2])
        kai = sb("kai", [C, NST])
        ke = sb("ke", [C, NST + 1])
        ks = sb("ks", [C, 16, NST + 1])
        ksc = sb("ksc", [C, NST + 1], I32)
        ksin = sb("ksin", [C, 2, NST])
        k4 = sb("k4", [C, 4, 2, NST])
        k4t = sb("k4t", [P, 4, C])
        lgrid = sb("lgrid", [P, NL])
        off_q = sb("off_q", [P, NL])
        off_r = sb("off_r", [P, NL])
        ph = sb("ph", [P, C, NL])
        turns = sb("turns", [P, C, NL])
        decay = sb("decay", [P, C, NJ + NI])
        fine = sb("fine", [P, C, NJ])
        coarse = sb("coarse", [P, C, NI])
        coarse2 = sb("coarse2", [P, C, NI])
        d_bc = sb("d_bc", [NI, C])
        last_p = sb("last_p", [NI, 1])
        k_sb = sb("k_sb", [NI, C, NJ])
        zeros = sb("zeros", [C, P])
        toep = sb("toep", [P, TBUF, T])
        yt = sb("yt", [P, 2, KC, TOK])
        yp = x_sb[:, 0:2 * KC, :].rearrange("p (two k) n -> p two k n", two=2)
        hid1 = x_sb[:, 2 * KC:2 * KC + 8, :]
        ot = c0

        bank = [ctx.enter_context(nc.psum_tensor(f"bank{i}", [P, 512], F32)) for i in range(8)]
        ps_h = bank[0:4]
        ps_c = bank[4:6]
        ps_f = bank[6:8]
        ps_y = bank[0:2]
        ps_u = bank[2:6]
        ps_o = bank[6:8]

        s_idx = sem("s_idx")
        s_seq = sem("s_seq")
        s_bs = sem("s_bs")
        s_w2 = sem("s_w2")
        s_x = [sem(f"s_x{i}") for i in range(NG)]
        s_wb = sem("s_wb")
        s_ar = sem("s_ar")
        s_bb = sem("s_bb")
        s_kin = sem("s_kin")
        s_l1 = sem("s_l1")
        s_dbc = sem("s_dbc")
        s_cst = sem("s_cst")
        s_idn = sem("s_idn")
        s_z0 = sem("s_z0")
        s_row = sem("s_row")
        s_wg = [sem(f"s_wg{i}") for i in range(NG)]
        s_wbd = sem("s_wbd")
        s_ohe = sem("s_ohe")
        s_yrow = sem("s_yrow")
        s_hd = sem("s_hd")
        s_hg = sem("s_hg")
        s_hu = sem("s_hu")
        s_cv = sem("s_cv")
        s_c0 = sem("s_c0")
        s_fd = [sem(f"s_fd{i}") for i in range(2)]
        s_ff = [sem(f"s_ff{i}") for i in range(2)]
        s_hw = sem("s_hw")
        s_hwt = sem("s_hwt")
        s_u = sem("s_u")
        s_ka = sem("s_ka")
        s_kb = sem("s_kb")
        s_k4 = sem("s_k4")
        s_kt = sem("s_kt")
        s_ks = sem("s_ks")
        s_kr = sem("s_kr")
        s_tp = [sem(f"s_tp{i}") for i in range(TBUF)]
        s_cd = sem("s_cd")
        s_ye = sem("s_ye")
        s_ys = [sem(f"s_ys{g}") for g in range(NT)]
        s_yg = [sem(f"s_yg{g}") for g in range(NT)]
        s_ud = sem("s_ud")
        s_ug = sem("s_ug")
        s_od = sem("s_od")
        s_oe = sem("s_oe")
        s_res = [sem(f"s_res{g}") for g in range(NT)]
        s_add = [sem(f"s_add{g}") for g in range(NT)]
        s_lr3 = sem("s_lr3")
        s_hw3 = sem("s_hw3")
        s_kd = sem("s_kd")
        s_dch = sem("s_dch")

        names = ["bias"]
        for g in range(NT):
            names += ([f"lr{g}0", f"lr{g}1"] if g < NT - 1 else []) + [f"hw{g}"] + (["k4"] if g == 1 else [])
            names += [f"oc{g}{i}" for i in range(KC)]
        unit = {n: i for i, n in enumerate(names)}

        def ring(n):
            return ps_f[unit[n] % 2]

        def wait_filled(eng, n):
            eng.wait_ge(s_fd[unit[n] % 2], unit[n] // 2 + 1)

        def wait_free(eng, n):
            if unit[n] >= 2:
                eng.wait_ge(s_ff[unit[n] % 2], unit[n] // 2)

        def filled(ins, n):
            ins.then_inc(s_fd[unit[n] % 2], 1)

        def freed(ins, n):
            ins.then_inc(s_ff[unit[n] % 2], 1)

        sess_even_odd = sess_id.rearrange("(one b) -> one b", one=1)

        block = ctx.enter_context(nc.Block())

        @block.sync
        def _(sp):
            sp.dma_start(sc_w[:, :], bass.AP(tensor=sess_chan_by4.tensor, offset=0, ap=[[2 * NG, BPG], [0, C], [1, 2 * NG]])
                         ).then_inc(s_idx, 16)
            xg = x.rearrange("(g b) c t -> g (b c) t", b=BPG)
            for i in range(GPT):
                sp.dma_start(x_sb[:, i, :], xg[i]).then_inc(s_x[i], 16)
            sp.wait_ge(s_z0, 1)
            for i in range(2):
                sp.dma_start(w2_bd[HID * i:HID * (i + 1), C * i:C * (i + 1)], w2).then_inc(s_w2, 16)
            sp.dma_start(ar_t[:, :, :], low_router_t.rearrange("(k p) n -> p k n", p=P)).then_inc(s_ar, 16)
            sp.dma_start(b2_row[:, :], b2.rearrange("(one s) -> one s", one=1).broadcast_to([P, C])).then_inc(s_w2, 16)
            sp.dma_start(seq_sb[:, :], seq_len.rearrange("(one b) -> one b", one=1).broadcast_to([P, B])).then_inc(s_seq, 16)
            sp.dma_start(clen_sb[:, :], conv_len.rearrange("(one b) -> one b", one=1).broadcast_to([P, B])).then_inc(s_seq, 16)
            sp.dma_start(wb_t[:, :, :], w_base_t.rearrange("(k p) o -> p k o", p=P)).then_inc(s_wb, 16)
            sp.dma_start(b_t[:, :], lora_b_t).then_inc(s_wb, 16)
            sp.dma_start(bb_col[:, :], b_base_c).then_inc(s_bb, 16)
            for i in range(GPT, NG):
                sp.dma_start(x_sb[:, i, :], xg[i]).then_inc(s_x[i], 16)
            sp.dma_start(up_sb[:, :, :], up.rearrange("(q h) d m -> (h d) q m", h=4)).then_inc(s_l1, 16)
            sp.dma_start(down_sb[:, :, :], down.rearrange("h m d -> m h d")).then_inc(s_l1, 16)
            sp.dma_start(k_rev[:, T:KLEN], zeros[:, :]).then_inc(s_kr, 16)
            sp.wait_ge(s_ks, 1)
            sp.dma_start(k_rev[:, 0:T].rearrange("h (i j) -> i h j", j=NJ), k_sb[:, :, :]).then_inc(s_kr, 16)
            sp.wait_ge(s_kr, 32)

            def load_toeplitz(g):
                for h in range(CPT * g, CPT * (g + 1)):
                    if h >= TBUF:
                        sp.wait_ge(s_cd, h - TBUF + 1)
                    src = bass.AP(tensor=k_rev, offset=h * KLEN, ap=[[1, P], [1, T]])
                    sp.dma_start(toep[:, h % TBUF, :], src).then_inc(s_tp[h % TBUF], 16)

            def store_rows(g):
                sp.wait_ge(s_ye, (g + 1) * CPT // 2)
                sp.dma_start(y_rows[g][:, :].rearrange("(k p) n -> p k n", p=P), yt[:, g % 2, :, :]).then_inc(s_ys[g], 16)

            def store_residual(g):
                sp.dma_start(out_rows[T * g:T * (g + 1), :].rearrange("(k p) n -> p k n", p=P),
                             u[:, :, CPT * g:CPT * (g + 1), :].rearrange("p k h b -> p k (h b)")).then_inc(s_res[g], 16)

            load_toeplitz(0)
            for b in range(2):
                n = max(unit[f"oc{NT - 1}{i}"] for i in range(KC) if unit[f"oc{NT - 1}{i}"] % 2 == b)
                sp.wait_ge(s_ff[b], n // 2 + 1)
            load_toeplitz(1)
            store_rows(0)
            store_residual(0)
            load_toeplitz(2)
            store_rows(1)
            store_residual(1)
            load_toeplitz(3)
            store_rows(2)
            store_residual(2)
            store_rows(3)
            store_residual(3)

        @block.gpsimd
        def _(pool):
            nc.gpsimd.memset(w2_bd[:, :], 0.0)
            nc.gpsimd.memset(zeros[:, :], 0.0).then_inc(s_z0, 1)
            nc.gpsimd.iota(p_int[:, :], [[0, 1]], base=0, channel_multiplier=1)
            nc.gpsimd.iota(p_col[:, :], [[0, 1]], base=0, channel_multiplier=1, allow_small_or_imprecise_dtypes=True)
            nc.gpsimd.iota(step_of[:, :], [[P, KC]], base=0, channel_multiplier=1, allow_small_or_imprecise_dtypes=True)
            nc.gpsimd.iota(rstep_of[:, :], [[P, KC]], base=P - 1, channel_multiplier=-1, allow_small_or_imprecise_dtypes=True)
            nc.gpsimd.iota(ramp[:, :], [[-1, NE]], base=NE, channel_multiplier=0, allow_small_or_imprecise_dtypes=True)
            nc.gpsimd.iota(lgrid[:, 0:NJ], [[-1, NJ]], base=NJ - 1, channel_multiplier=0, allow_small_or_imprecise_dtypes=True)
            nc.gpsimd.iota(lgrid[:, NJ:NL], [[0, 2], [-NJ, NI]], base=T - NJ, channel_multiplier=0,
                           allow_small_or_imprecise_dtypes=True).then_inc(s_cst, 1)
            nc.gpsimd.memset(ident[:, :], 0.0).then_inc(s_idn, 1)
            pool.wait_ge(s_idn, 1)
            nc.gpsimd.affine_select(out=ident[:, :], in_=ident[:, :], compare_op=ALU.not_equal, fill=1.0, base=0,
                                    pattern=[[-1, P]], channel_multiplier=1).then_inc(s_idn, 1)
            pool.wait_ge(s_row, 1)
            for i in range(NG):
                nc.gpsimd.indirect_dma_start(
                    out=w_raw[:, i, :], out_offset=None, in_=w_sess.rearrange("e c h -> (e c) h"),
                    in_offset=bass.IndirectOffsetOnAxis(ap=row_w[:, i:i + 1], axis=0)).then_inc(s_wg[i], 16)
            for n in range(NG):
                g, i = n // GPT, n % GPT
                pool.wait_ge(s_cv, n + 1)
                v = c0[:, g % 2, :, P * i:P * (i + 1)].rearrange("p k (b s) -> p k b s", s=C)
                m = tmask[:, :, BPG * n:BPG * (n + 1)].unsqueeze(3).broadcast_to([P, KC, BPG, C])
                nc.gpsimd.tensor_tensor(v, v, m, ALU.mult).then_inc(s_c0, 1)

            def gather(g):
                pool.wait_ge(s_ys[g], 16)
                if g >= 2:
                    pool.wait_ge(s_ud, KC * (g - 1))
                for q in range(KC):
                    nc.gpsimd.indirect_dma_start(
                        out=yp[:, g % 2, q, :], out_offset=None, in_=y_rows[g][:, :],
                        in_offset=bass.IndirectOffsetOnAxis(ap=yrow_sb[:, q:q + 1], axis=0)).then_inc(s_yg[g], 16)

            def add_out(g):
                if g == 0:
                    for r in range(NT):
                        pool.wait_ge(s_res[r], 16)
                for q in range(KC):
                    pool.wait_ge(s_oe, KC * g + q + 1)
                    nc.gpsimd.indirect_dma_start(
                        out=out_rows, out_offset=bass.IndirectOffsetOnAxis(ap=orow_sb[:, g, q:q + 1], axis=0),
                        in_=ot[:, g % 2, q, :], in_offset=None, compute_op=ALU.add).then_inc(s_add[g], 16)

            pool.wait_ge(s_yrow, 1)
            gather(0)
            gather(1)
            add_out(0)
            gather(2)
            add_out(1)
            gather(3)
            add_out(2)
            add_out(3)
            for g in range(NT):
                pool.wait_ge(s_add[g], 16 * KC)

        @block.scalar
        def _(act):
            act.dma_start(sid_e[:, :], sess_even_odd.broadcast_to([NS, B])).then_inc(s_bs, 16)
            act.dma_start(bs_sb[:, :], b_sess).then_inc(s_bs, 16)
            act.dma_start(kz[:, 0:NST], log_a_re).then_inc(s_kin, 16)
            act.dma_start(kz[:, NST:NST + 1], log_dt.rearrange("(h one) -> h one", one=1)).then_inc(s_kin, 16)
            act.dma_start(kai[:, :], a_im).then_inc(s_kin, 16)
            act.dma_start(kc[:, :, :], c_ri).then_inc(s_kin, 16)
            act.dma_start(perm_sb[:, :], perm_c).then_inc(s_l1, 16)
            act.dma_start(d_bc[:, :], d_skip.rearrange("(one h) -> one h", one=1).broadcast_to([NI, C])).then_inc(s_dbc, 16)

            def gelus(g):
                for j in range(PAIRS):
                    n = PAIRS * g + j
                    act.wait_ge(s_hd, n + 1)
                    if n >= 4:
                        act.wait_ge(s_hu, n // 2 - 1)
                    nc.scalar.activation(hid0[:, n % 4, :], ps_h[n % 4][:, :], ACT.Gelu,
                                         bias=bias_h[:, n:n + 1]).then_inc(s_hg, 1)

            act.wait_ge(s_ff[unit["bias"] % 2], 1)
            gelus(0)
            act.wait_ge(s_bb, 16)
            for g in range(NT):
                if g + 1 < NT:
                    gelus(g + 1)
                wait_filled(act, f"hw{g}")
                ins = nc.scalar.copy(hw_t[:, :], ring(f"hw{g}")[:, :])
                freed(ins, f"hw{g}")
                if g == 0:
                    act.wait_ge(s_ka, 1)
                    nc.scalar.activation(ksin[:, 0, :], ks[:, 5, 0:NST], ACT.Sin)
                    nc.scalar.activation(ksin[:, 1, :], ks[:, 5, 0:NST], ACT.Sin, scale=0.5).then_inc(s_kb, 1)
                for i in range(KC):
                    wait_filled(act, f"oc{g}{i}")
                    ins = nc.scalar.activation(
                        u[:, i, :, BPT * g:BPT * (g + 1)].rearrange("p s b -> p b s"),
                        ring(f"oc{g}{i}")[:, :].rearrange("p (b s) -> p b s", s=C), ACT.Identity, bias=bb_col[:, i:i + 1])
                    freed(ins, f"oc{g}{i}")
                    if g == 2 and i == 1:
                        act.wait_ge(s_ka, 2)
                        nc.scalar.activation(turns[:, :, :], ph[:, :, :], ACT.Sin)
                        nc.scalar.activation(decay[:, :, :], decay[:, :, :], ACT.Exp).then_inc(s_kb, 1)
            for n in range(NT * NH):
                q = n // 4
                act.wait_ge(s_ud, q + 1)
                if q >= 2:
                    act.wait_ge(s_od, q - 1)
                nc.scalar.activation(hid1[:, n % 8, :], ps_u[n % 4][:, :], ACT.Gelu).then_inc(s_ug, 1)

        @block.vector
        def _(dve):
            V = nc.vector
            chain = [0]

            def link(ins):
                chain[0] += 1
                ins.then_inc(s_dch, 1)
                dve.wait_ge(s_dch, chain[0])

            dve.wait_ge(s_cst, 1)
            link(V.tensor_scalar(chan_int[:, :], p_int[:, :], C - 1, None, ALU.bitwise_and))
            link(V.tensor_scalar(par_int[:, :], p_int[:, :], 5, 1, ALU.logical_shift_right, ALU.bitwise_and))
            link(V.tensor_copy(chan_of_p[:, :], chan_int[:, :]))
            link(V.tensor_copy(parity[:, 1:2], par_int[:, :]))
            dve.wait_ge(s_idx, 16)
            V.tensor_scalar(row_w[:, :], sc_w[:, 0:NG], float(C), chan_of_p[:, 0:1], ALU.mult, ALU.add).then_inc(s_row, 1)
            link(V.tensor_scalar(parity[:, 0:1], parity[:, 1:2], -1.0, 1.0, ALU.mult, ALU.add))
            link(V.tensor_scalar(cmask[:, :], sc_w[:, NG:2 * NG], chan_of_p[:, 0:1], None, ALU.is_gt))
            link(V.tensor_tensor(cmask2[:, :, :], cmask[:, :].unsqueeze(2).broadcast_to([P, NG, 2]),
                                 parity[:, :].unsqueeze(1).broadcast_to([P, NG, 2]), ALU.mult))
            dve.wait_ge(s_bs, 32)
            V.tensor_scalar(onehot_e[:, :, :], sid_e[:, :].rearrange("e (b two) -> e two b", two=2), p_col[0:NS, 0:1], None,
                            ALU.is_equal).then_inc(s_ohe, 1)
            def exp_small(dst_p, dst_scale, z, tmp_k, tmp_r):
                link(V.tensor_scalar(tmp_k, z, LOG2E, ROUND, ALU.mult, ALU.add))
                link(V.tensor_scalar(tmp_k, tmp_k, ROUND, -126.0, ALU.subtract, ALU.max))
                link(V.scalar_tensor_tensor(tmp_r, tmp_k, -LN2_HI, z, ALU.mult, ALU.add))
                link(V.scalar_tensor_tensor(tmp_r, tmp_k, -LN2_LO, tmp_r, ALU.mult, ALU.add))
                V.tensor_scalar(dst_scale, tmp_k, 127.0, 2.0 ** 23, ALU.add, ALU.mult)
                link(V.tensor_scalar(dst_p, tmp_r, EXP_COEFFS[0], None, ALU.mult))
                for c in EXP_COEFFS[1:]:
                    link(V.scalar_tensor_tensor(dst_p, dst_p, c, tmp_r, ALU.add, ALU.mult))

            N1 = NST + 1
            re, im = k4[:, 0, 0, :], k4[:, 1, 0, :]
            em1, ex = ks[:, 6, 0:NST], ks[:, 7, 0:NST]

            def kernel_phases():
                dve.wait_ge(s_kin, 64)
                exp_small(ks[:, 2, 0:N1], ksc[:, 0:N1], kz[:, :], ks[:, 0, 0:N1], ks[:, 1, 0:N1])
                link(V.scalar_tensor_tensor(ke[:, :], ks[:, 2, 0:N1], 1.0, ksc[:, 0:N1].bitcast(F32), ALU.add, ALU.mult))
                dt = ke[:, NST:N1]
                link(V.tensor_scalar(re, ke[:, 0:NST], dt, -1.0, ALU.mult, ALU.mult))
                link(V.tensor_scalar(im, kai[:, :], dt, None, ALU.mult))
                link(V.tensor_scalar(ks[:, 4, 0:NST], im, 1.0 / (4 * HALF_PI), ROUND, ALU.mult, ALU.add))
                link(V.tensor_scalar(ks[:, 4, 0:NST], ks[:, 4, 0:NST], ROUND, None, ALU.subtract))
                src = im
                for part in TWO_PI_PARTS:
                    link(V.scalar_tensor_tensor(ks[:, 5, 0:NST], ks[:, 4, 0:NST], -part, src, ALU.mult, ALU.add))
                    src = ks[:, 5, 0:NST]
                V.tensor_scalar(ks[:, 5, 0:NST], src, -PI_BELOW, PI_BELOW, ALU.max, ALU.min).then_inc(s_ka, 1)

            def kernel_params():
                link(V.tensor_scalar(kz[:, 0:NST], re, -87.0, None, ALU.max))
                exp_small(ks[:, 2, 0:NST], ksc[:, 0:NST], kz[:, 0:NST], ks[:, 0, 0:NST], ks[:, 1, 0:NST])
                scale = ksc[:, 0:NST].bitcast(F32)
                link(V.tensor_scalar(ks[:, 3, 0:NST], scale, 1.0, None, ALU.subtract))
                link(V.tensor_tensor(em1, ks[:, 2, 0:NST], scale, ALU.mult))
                link(V.tensor_tensor(em1, em1, ks[:, 3, 0:NST], ALU.add))
                link(V.tensor_scalar(ex, em1, 1.0, None, ALU.add))
                dve.wait_ge(s_kb, 1)
                er, ei = ks[:, 8, 0:NST], ks[:, 9, 0:NST]
                link(V.tensor_tensor(ei, ex, ksin[:, 0, :], ALU.mult))
                link(V.tensor_tensor(er, ksin[:, 1, :], ksin[:, 1, :], ALU.mult))
                link(V.tensor_tensor(er, er, ex, ALU.mult))
                link(V.scalar_tensor_tensor(er, er, -2.0, em1, ALU.mult, ALU.add))
                cr, ci = kc[:, :, 0], kc[:, :, 1]
                nr, ni, t1 = ks[:, 10, 0:NST], ks[:, 11, 0:NST], ks[:, 12, 0:NST]
                link(V.tensor_tensor(nr, cr, er, ALU.mult))
                link(V.tensor_tensor(t1, ci, ei, ALU.mult))
                link(V.tensor_tensor(nr, nr, t1, ALU.subtract))
                link(V.tensor_tensor(ni, cr, ei, ALU.mult))
                link(V.tensor_tensor(t1, ci, er, ALU.mult))
                link(V.tensor_tensor(ni, ni, t1, ALU.add))
                ar, ai, inv = ks[:, 13, 0:NST], kai[:, :], ks[:, 14, 0:NST]
                link(V.tensor_scalar(ar, ke[:, 0:NST], -1.0, None, ALU.mult))
                link(V.tensor_tensor(inv, ar, ar, ALU.mult))
                link(V.tensor_tensor(t1, ai, ai, ALU.mult))
                link(V.tensor_tensor(inv, inv, t1, ALU.add))
                link(V.reciprocal(inv, inv))
                link(V.tensor_tensor(t1, nr, ar, ALU.mult))
                link(V.tensor_tensor(er, ni, ai, ALU.mult))
                link(V.tensor_tensor(t1, t1, er, ALU.add))
                link(V.tensor_tensor(ei, ni, ar, ALU.mult))
                link(V.tensor_tensor(er, nr, ai, ALU.mult))
                link(V.tensor_tensor(ei, ei, er, ALU.subtract))
                link(V.scalar_tensor_tensor(k4[:, 2, 0, :], t1, 2.0, inv, ALU.mult, ALU.mult))
                link(V.scalar_tensor_tensor(k4[:, 2, 1, :], ei, -2.0, inv, ALU.mult, ALU.mult))
                V.tensor_copy(k4[:, 0, 1, :], re)
                V.tensor_copy(k4[:, 1, 1, :], im)
                V.tensor_copy(k4[:, 3, 0, :], k4[:, 2, 1, :])
                V.tensor_scalar(k4[:, 3, 1, :], k4[:, 2, 0, :], -1.0, None, ALU.mult).then_inc(s_k4, 1)

            def weights(n):
                dve.wait_ge(s_wg[n], 16)
                V.tensor_tensor(w_bd[:, n, :, :], w_raw[:, n, :].unsqueeze(1).broadcast_to([P, 2, HID]),
                                cmask2[:, n, :].unsqueeze(2).broadcast_to([P, 2, HID]), ALU.mult).then_inc(s_wbd, 1)

            wait_filled(dve, "bias")
            ins = V.tensor_copy(bias_h[:, :], ring("bias")[:, 0:B // 2])
            freed(ins, "bias")
            def cond_out(n):
                g, i = n // GPT, n % GPT
                if n == 0:
                    dve.wait_ge(s_w2, 48)
                dve.wait_ge(s_hu, n + 1)
                if g >= 2 and i == 0:
                    wait_filled(dve, f"oc{g - 2}{KC - 1}")
                V.tensor_tensor(c0[:, g % 2, :, P * i:P * (i + 1)].rearrange("p k (b s) -> p k b s", s=C),
                                ps_c[n % 2][:, :].rearrange("p (k b s) -> p k b s", k=KC, s=C),
                                b2_row[:, :].unsqueeze(1).unsqueeze(1).broadcast_to([P, KC, BPG, C]), ALU.add).then_inc(s_cv, 1)

            def low_rank(g, i):
                return ps_h[i] if g == NT - 1 else ring(f"lr{g}{i}")

            def wide(a):
                return a.unsqueeze(2).broadcast_to([P, GPT, NE])

            ramps = ramp[:, :].unsqueeze(1).broadcast_to([P, GPT, NE])

            def top(logits, m, first, hot):
                link(V.tensor_reduce(rs[:, m, :], logits, AX_X, ALU.max))
                link(V.tensor_tensor(rt[:, 0], logits, wide(rs[:, m, :]), ALU.is_equal))
                link(V.tensor_tensor(rt[:, 0], rt[:, 0], ramps, ALU.mult))
                link(V.tensor_reduce(rs[:, first, :], rt[:, 0], AX_X, ALU.max))
                link(V.tensor_tensor(rt[:, hot], ramps, wide(rs[:, first, :]), ALU.is_equal))

            def route_top(g):
                for i in range(2):
                    if g == NT - 1:
                        dve.wait_ge(s_lr3, i + 1)
                    else:
                        wait_filled(dve, f"lr{g}{i}")
                    link(V.tensor_copy(lg[:, 2 * i:2 * i + 2, :],
                                       low_rank(g, i)[:, 0:2 * LR].rearrange("p (s n) -> p s n", n=LR)[:, :, P:LR]))
                top(lg[:, :, :], 0, 4, 1)
                link(V.scalar_tensor_tensor(rt[:, 2], rt[:, 1], -BIG, lg[:, :, :], ALU.mult, ALU.add))
                top(rt[:, 2], 1, 5, 3)

            def route_exp(g):
                link(V.tensor_tensor(rs[:, 2, :], rs[:, 1, :], rs[:, 0, :], ALU.subtract))
                link(V.tensor_scalar(rs[:, 2, :], rs[:, 2, :], -87.0, None, ALU.max))
                exp_small(re_[:, 2, :], re_i[:, :], rs[:, 2, :], re_[:, 0, :], re_[:, 1, :])
                link(V.scalar_tensor_tensor(rs[:, 3, :], re_[:, 2, :], 1.0, re_i[:, :].bitcast(F32), ALU.add, ALU.mult))

            def route_weights(g):
                link(V.tensor_scalar(rs[:, 6, :], rs[:, 3, :], 0.5, 0.5, ALU.mult, ALU.add))
                link(V.reciprocal(rs[:, 6, :], rs[:, 6, :]))
                link(V.tensor_tensor(rs[:, 7, :], rs[:, 6, :], rs[:, 3, :], ALU.mult))
                link(V.tensor_tensor(rt[:, 1], rt[:, 1], wide(rs[:, 6, :]), ALU.mult))
                link(V.tensor_tensor(rt[:, 3], rt[:, 3], wide(rs[:, 7, :]), ALU.mult))
                link(V.tensor_tensor(rt[:, 4], rt[:, 1], rt[:, 3], ALU.add))
                if g >= 1:
                    wait_filled(dve, f"hw{g - 1}")
                for i in range(2):
                    ins = V.tensor_tensor(
                        hw[:, 2 * i:2 * i + 2, :].rearrange("p s (e r) -> p s e r", e=NE),
                        low_rank(g, i)[:, 0:2 * LR].rearrange("p (s n) -> p s n", n=LR)[:, :, 0:P].rearrange("p s (e r) -> p s e r", e=NE),
                        rt[:, 4, 2 * i:2 * i + 2, :].unsqueeze(3).broadcast_to([P, 2, NE, RANK]), ALU.mult)
                    if g == NT - 1:
                        ins.then_inc(s_hw3, 1)
                    else:
                        freed(ins, f"lr{g}{i}")

            def kernel_tables():
                wait_filled(dve, "k4")
                ins = V.tensor_copy(k4t[:, :, :], ring("k4")[:, 0:4 * C].rearrange("p (a h) -> p a h", a=4))
                freed(ins, "k4")
                dve.wait_ge(s_ff[unit["k4"] % 2], unit["k4"] // 2 + 1)
                for t, v in ((off_q, 0.25), (off_r, HALF_PI)):
                    V.tensor_scalar(t[:, 0:NJ], p_col[:, :].broadcast_to([P, NJ]), P / 2.0, v, ALU.is_lt, ALU.mult)
                    V.memset(t[:, NJ:NJ + NI], 0.0)
                    link(V.memset(t[:, NJ + NI:NL], v))
                lb = lgrid[:, :].unsqueeze(1).broadcast_to([P, C, NL])
                V.tensor_tensor(decay[:, :, :], k4t[:, 0, :].unsqueeze(2).broadcast_to([P, C, NJ + NI]),
                                lgrid[:, 0:NJ + NI].unsqueeze(1).broadcast_to([P, C, NJ + NI]), ALU.mult)
                link(V.tensor_tensor(ph[:, :, :], k4t[:, 1, :].unsqueeze(2).broadcast_to([P, C, NL]), lb, ALU.mult))
                link(V.scalar_tensor_tensor(turns[:, :, :], ph[:, :, :], 1.0 / (4 * HALF_PI),
                                            off_q[:, :].unsqueeze(1).broadcast_to([P, C, NL]), ALU.mult, ALU.add))
                link(V.tensor_scalar(turns[:, :, :], turns[:, :, :], ROUND, None, ALU.add))
                link(V.tensor_scalar(turns[:, :, :], turns[:, :, :], ROUND, None, ALU.subtract))
                for part in TWO_PI_PARTS:
                    link(V.scalar_tensor_tensor(ph[:, :, :], turns[:, :, :], -part, ph[:, :, :], ALU.mult, ALU.add))
                link(V.tensor_tensor(ph[:, :, :], ph[:, :, :], off_r[:, :].unsqueeze(1).broadcast_to([P, C, NL]), ALU.add))
                V.tensor_scalar(ph[:, :, :], ph[:, :, :], -PI_BELOW, PI_BELOW, ALU.max, ALU.min).then_inc(s_ka, 1)

            def kernel_factors():
                dve.wait_ge(s_kb, 2)
                sines = turns
                link(V.tensor_tensor(coarse[:, :, :], sines[:, :, NJ + NI:NL],
                                     k4t[:, 2, :].unsqueeze(2).broadcast_to([P, C, NI]), ALU.mult))
                link(V.tensor_tensor(coarse2[:, :, :], sines[:, :, NJ:NJ + NI],
                                     k4t[:, 3, :].unsqueeze(2).broadcast_to([P, C, NI]), ALU.mult))
                link(V.tensor_tensor(coarse[:, :, :], coarse[:, :, :], coarse2[:, :, :], ALU.add))
                link(V.tensor_tensor(coarse[:, :, :], coarse[:, :, :], decay[:, :, NJ:NJ + NI], ALU.mult))
                V.tensor_tensor(fine[:, :, :], sines[:, :, 0:NJ], decay[:, :, 0:NJ], ALU.mult).then_inc(s_kt, 1)

            def kernel_out():
                dve.wait_ge(s_dbc, 16)
                link(V.tensor_scalar(last_p[:, :], p_col[0:NI, :], float(NI - 1), None, ALU.is_equal))
                link(V.tensor_scalar(d_bc[:, :], d_bc[:, :], last_p[:, 0:1], None, ALU.mult))
                HALF = C // 2
                for i in range(2):
                    dve.wait_ge(s_kd, i + 1)
                    link(V.tensor_copy(k_sb[:, HALF * i:HALF * (i + 1), :],
                                       ps_c[i][0:NI, :].rearrange("p (h j) -> p h j", j=NJ)))
                V.tensor_tensor(k_sb[:, :, NJ - 1], k_sb[:, :, NJ - 1], d_bc[:, :], ALU.add).then_inc(s_ks, 1)

            for n in range(GPT):
                weights(n)
            dve.wait_ge(s_seq, 32)
            V.tensor_tensor(tmask[:, :, :], step_of[:, :].unsqueeze(2).broadcast_to([P, KC, B]),
                            seq_sb[:, :].unsqueeze(1).broadcast_to([P, KC, B]), ALU.is_lt)
            V.tensor_tensor(lmask[:, :, :], rstep_of[:, :].unsqueeze(2).broadcast_to([P, KC, B]),
                            clen_sb[:, :].unsqueeze(1).broadcast_to([P, KC, B]), ALU.is_lt)
            kernel_phases()
            for n in range(GPT):
                cond_out(n)
            dve.wait_ge(s_l1, 48)
            link(V.tensor_scalar(yrow_sb[:, :], perm_sb[:, :], P - 1, None, ALU.bitwise_xor))
            for g in range(NT):
                last = V.tensor_scalar(orow_sb[:, g, :], perm_sb[:, :], float(T * g), None, ALU.add)
            last.then_inc(s_yrow, 1)
            for g in range(NT):
                if g + 1 < NT:
                    for n in range(GPT * (g + 1), GPT * (g + 2)):
                        weights(n)
                route_top(g)
                if g + 1 < NT:
                    cond_out(GPT * (g + 1))
                route_exp(g)
                if g + 1 < NT:
                    cond_out(GPT * (g + 1) + 1)
                route_weights(g)
                if g + 1 < NT:
                    cond_out(GPT * (g + 1) + 2)
                    cond_out(GPT * (g + 1) + 3)
                if g == 0:
                    kernel_params()
                if g == 1:
                    kernel_tables()
                if g == 2:
                    kernel_factors()
            kernel_out()

            def conv_out(n):
                g, j = n // (CPT // 2), n % (CPT // 2)
                if g >= 2 and j == 0:
                    dve.wait_ge(s_ys[g - 2], 16)
                dve.wait_ge(s_cd, 2 * (n + 1))
                for i in range(2):
                    last = V.tensor_tensor(
                        yt[:, g % 2, :, B * (2 * j + i):B * (2 * j + i + 1)],
                        ps_y[n % 2][:, KC * B * i:KC * B * (i + 1)].rearrange("p (k b) -> p k b", k=KC),
                        lmask[:, :, :], ALU.mult)
                last.then_inc(s_ye, 1)

            def heads_out(n):
                g, q = n // KC, n % KC
                dve.wait_ge(s_od, n + 1)
                if g >= 2 and q == 0:
                    dve.wait_ge(s_add[g - 2], 16 * KC)
                V.tensor_copy(ot[:, g % 2, q, :], ps_o[n % 2][:, :]).then_inc(s_oe, 1)

            for n in range(CPT):
                conv_out(n)
            for n in range(NT * KC):
                if CPT + n < C // 2:
                    conv_out(CPT + n)
                heads_out(n)

        @block.tensor
        def _(pe):
            mm = nc.tensor.matmul

            def cond_first(n):
                pe.wait_ge(s_x[n], 16)
                pe.wait_ge(s_wbd, n + 1)
                if n >= 2:
                    pe.wait_ge(s_hg, 2 * (n - 1))
                for i in range(2):
                    mm(ps_h[(2 * n + i) % 4][:, :], w_bd[64 * i:64 * (i + 1), n, :, :], x_sb[64 * i:64 * (i + 1), n, :],
                       start=True, stop=True).then_inc(s_hd, 1)

            def cond(g):
                cond_first(GPT * g)
                for n in range(GPT * g, GPT * (g + 1)):
                    if n + 1 < GPT * (g + 1):
                        cond_first(n + 1)
                    pe.wait_ge(s_hg, 2 * (n + 1))
                    if n >= 2:
                        pe.wait_ge(s_cv, n - 1)
                    for i in range(2):
                        for k in range(KC):
                            o = P * k + 2 * C * i
                            last = mm(ps_c[n % 2][:, o:o + 2 * C], hid0[:, (2 * n + i) % 4, P * k:P * (k + 1)], w2_bd[:, :],
                                      start=True, stop=True)
                    last.then_inc(s_hu, 1)

            pe.wait_ge(s_ohe, 1)
            for i in range(2):
                last = mm(ring("bias")[HID * i:HID * (i + 1), 0:B // 2], bs_sb[:, :], onehot_e[:, i, :], start=True, stop=True)
            filled(last, "bias")
            pe.wait_ge(s_w2, 48)
            cond(0)
            pe.wait_ge(s_idn, 2)
            pe.wait_ge(s_ar, 16)

            def low_rank(g):
                for i in range(2):
                    if g == NT - 1:
                        acc = ps_h[i]
                        pe.wait_ge(s_hg, NG * 2)
                    else:
                        acc = ring(f"lr{g}{i}")
                        wait_free(pe, f"lr{g}{i}")
                    for s in range(2):
                        pe.wait_ge(s_c0, GPT * g + 2 * i + s + 1)
                        for k in range(KC):
                            last = mm(acc[:, LR * s:LR * (s + 1)], c0[:, g % 2, k, P * (2 * i + s):P * (2 * i + s + 1)],
                                      ar_t[:, k, :], start=(k == 0), stop=(k == KC - 1))
                    if g == NT - 1:
                        last.then_inc(s_lr3, 1)
                    else:
                        filled(last, f"lr{g}{i}")

            def low_rank_turned(g):
                if g == NT - 1:
                    pe.wait_ge(s_hw3, 2)
                else:
                    for i in range(2):
                        pe.wait_ge(s_ff[unit[f"lr{g}{i}"] % 2], unit[f"lr{g}{i}"] // 2 + 1)
                wait_free(pe, f"hw{g}")
                for s in range(GPT):
                    last = nc.tensor.transpose(ring(f"hw{g}")[:, P * s:P * (s + 1)], hw[:, s, :], ident[:, :])
                filled(last, f"hw{g}")

            def linear(g, i):
                acc = ring(f"oc{g}{i}")
                wait_free(pe, f"oc{g}{i}")
                for s in range(GPT):
                    mm(acc[:, P * s:P * (s + 1)], x_sb[:, GPT * g + s, P * i:P * (i + 1)], ident[:, :],
                       start=(s == 0), stop=False, is_transpose=True, skip_group_check=True)
                for k in range(KC):
                    mm(acc[:, :], wb_t[:, k, P * i:P * (i + 1)], c0[:, g % 2, k, :], start=False, stop=False,
                       skip_group_check=True)
                if i == 0:
                    pe.wait_ge(s_ff[unit[f"hw{g}"] % 2], unit[f"hw{g}"] // 2 + 1)
                last = mm(acc[:, :], b_t[:, P * i:P * (i + 1)], hw_t[:, :], start=False, stop=True, skip_group_check=True)
                filled(last, f"oc{g}{i}")

            for g in range(NT - 1):
                low_rank(g)
                cond(g + 1)
                low_rank_turned(g)
                if g == 0:
                    pe.wait_ge(s_wb, 32)
                if g == 1:
                    pe.wait_ge(s_k4, 1)
                    wait_free(pe, "k4")
                    for a in range(4):
                        last = nc.tensor.transpose(ring("k4")[:, C * a:C * (a + 1)],
                                                   k4[:, a, :, :].rearrange("h c n -> h (c n)"), ident[0:C, 0:C])
                    filled(last, "k4")
                linear(g, 0)
                linear(g, 1)
                if g == NT - 2:
                    low_rank(NT - 1)
                linear(g, 2)
                linear(g, 3)
            pe.wait_ge(s_kt, 1)
            pe.wait_ge(s_cv, NG)
            for i in range(2):
                for h in range(C // 2):
                    hh = C // 2 * i + h
                    last = mm(ps_c[i][0:NI, NJ * h:NJ * (h + 1)], coarse[:, hh, :], fine[:, hh, :], start=True, stop=True)
                last.then_inc(s_kd, 1)
            low_rank_turned(NT - 1)
            for i in range(KC):
                linear(NT - 1, i)

            def conv(h):
                pe.wait_ge(s_tp[h % TBUF], 16 * (h // TBUF + 1))
                if h % 2 == 0 and h >= 4:
                    pe.wait_ge(s_ye, h // 2 - 1)
                acc = ps_y[(h // 2) % 2][:, KC * B * (h % 2):KC * B * (h % 2 + 1)]
                for d in range(KC):
                    last = mm(acc[:, B * d:KC * B], toep[:, h % TBUF, P * (KC - 1 - d):P * (KC - d)],
                              u[:, 0:KC - d, h, :], start=(d == 0), stop=(d == KC - 1), skip_group_check=True)
                last.then_inc(s_cd, 1)

            def rises(n):
                g, q = n // KC, n % KC
                if q == 0:
                    pe.wait_ge(s_yg[g], 16 * KC)
                if n >= 1:
                    pe.wait_ge(s_ug, 4 * n)
                for i in range(4):
                    last = mm(ps_u[i][:, :], up_sb[DH * i:DH * (i + 1), q, :], yp[DH * i:DH * (i + 1), g % 2, q, :],
                              start=True, stop=True)
                last.then_inc(s_ud, 1)

            def falls(n):
                g, q = n // KC, n % KC
                pe.wait_ge(s_ug, 4 * (n + 1))
                if n >= 2:
                    pe.wait_ge(s_oe, n - 1)
                for i in range(4):
                    last = mm(ps_o[n % 2][DH * i:DH * (i + 1), :], down_sb[:, 4 * q + i, :], hid1[:, (4 * n + i) % 8, :],
                              start=True, stop=True)
                last.then_inc(s_od, 1)

            for b in range(2):
                n = max(unit[f"oc{NT - 1}{i}"] for i in range(KC) if unit[f"oc{NT - 1}{i}"] % 2 == b)
                pe.wait_ge(s_ff[b], n // 2 + 1)
            pe.wait_ge(s_l1, 48)
            for h in range(2 * CPT):
                conv(h)
            rises(0)
            for n in range(NT * KC):
                if n < CPT:
                    conv(2 * CPT + 2 * n)
                    conv(2 * CPT + 2 * n + 1)
                if n + 1 < NT * KC:
                    rises(n + 1)
                falls(n)


def kernel(**inputs):
    import numpy as _np
    import concourse.bacc as _bacc
    from concourse import mybir as _mybir
    from concourse.bass_utils import run_bass_kernel_spmd as _run

    v = {name: _np.asarray(a) for name, a in inputs.items()}
    low = v["L0_ffn_A"].reshape(-1, v["L0_ffn_A"].shape[2])
    laid_out = {
        "x": v["x"],
        "sess_id": v["itok_B_0_7"],
        "sess_chan_by4": _np.concatenate([v["itok_B_0_7"].reshape(-1, 4).T, v["_lenS"].reshape(-1, 4).T], axis=1),
        "seq_len": v["itok_B_2182_4065"],
        "conv_len": v["itok_B_8_3872"],
        "w_sess": v["L0_cond_W_sess"],
        "b_sess": v["L0_cond_b_sess"],
        "w2": v["L0_cond_W2"],
        "b2": v["L0_cond_b2"],
        "w_base_t": v["L0_ffn_W_base"].T,
        "b_base_c": v["L0_ffn_b_base"].reshape(-1, 128).T,
        "low_router_t": _np.concatenate([low, v["L0_ffn_W_router"]]).T,
        "lora_b_t": v["L0_ffn_B"].transpose(0, 2, 1).reshape(low.shape[0], -1),
        "log_dt": v["L1_cond_log_dt"],
        "c_ri": v["L1_cond_C"],
        "log_a_re": v["L1_cond_log_A_real"],
        "a_im": v["L1_cond_A_imag"],
        "d_skip": v["L1_cond_D"],
        "up": v["L1_ffn_up"],
        "down": v["L1_ffn_down"],
        "perm_c": v["L1_ffn_perm"].reshape(-1, 128).T,
    }
    nc = _bacc.Bacc("TRN2", target_bir_lowering=False, num_devices=1)
    arrays, args = {}, []
    for name, a in laid_out.items():
        a = _np.ascontiguousarray(a)
        arrays[f"in_{name}"] = a
        args.append(nc.dram_tensor(f"in_{name}", a.shape, _mybir.dt.from_np(a.dtype), kind="ExternalInput").ap())
    batches, channels, steps = v["x"].shape
    res = nc.dram_tensor("out_dram", (4, steps, channels // 4, batches), _mybir.dt.float32, kind="ExternalOutput").ap()
    adaln_ffn_kernel(nc, *args, res)
    r = _run(nc, [arrays], core_ids=[0])
    return r.results[0]["out_dram"].transpose(3, 0, 2, 1).reshape(batches, channels, steps)
```

```python
from contextlib import ExitStack

import concourse.bass as bass
from concourse import mybir

P = 128
ALU = mybir.AluOpType
ACT = mybir.ActivationFunctionType
F32 = mybir.dt.float32
F16 = mybir.dt.float16
BF16 = mybir.dt.bfloat16
I32 = mybir.dt.int32
AX_X = mybir.AxisListType.X

ROUND = 1.5 * 2.0 ** 23
LOG2E = 1.4426950408889634
LN2_HI, LN2_LO = 0.693359375, -2.12194440e-4
EXP_COEFFS = [1 / 5040, 1 / 720, 1 / 120, 1 / 24, 1 / 6, 1 / 2, 1.0]
TWO_PI_PARTS = (6.28125, 1.9340515136718750e-3, 1.2556660176e-6)
HALF_PI = 1.5707963267948966
PI_BELOW = 3.1415925
BIG = 3.0e38


def adaln_ffn_kernel(nc, x, x_steps, sess_id, sess_chan_by4, seq_len, conv_len, w_sess, b_sess, w2, b2, w_base_t, b_base_c,
                     low_router_t, lora_b_t, log_dt, c_ri, log_a_re, a_im, d_skip, up, down, perm_c, perm_h, out):
    B, C, T = x.shape
    NS, _, HID = w_sess.shape
    NE = low_router_t.shape[1] - P
    RANK = P // NE
    NST = a_im.shape[1]
    NH, DH, M = up.shape
    KC = T // P
    NT = B * C // T
    TOK = T
    BPG = P // C
    NG = B // BPG
    GPT = NG // NT
    BPT = B // NT
    PAIRS = BPT // 2
    LR = P + NE
    CPQ = C // 4
    NA = 2
    CPA = C // NA
    TOKA = CPA * B
    HQ = NH // 4
    SPLIT = NG // 2 + 1
    KLEN = T + P
    NI, NJ = 16, 32
    NL = NJ + 2 * NI

    k_rev = nc.dram_tensor("k_rev", [C, 2, KLEN], F16, kind="Internal")
    y_rows = [nc.dram_tensor(f"y_rows{a}", [2 * T, TOKA], F16, kind="Internal") for a in range(NA)]
    out_rows = out.rearrange("a t g h b -> (a t) (g h b)")

    with ExitStack() as ctx:
        def sb(name, shape, dt=F32):
            return ctx.enter_context(nc.sbuf_tensor(name, shape, dt))

        def sem(name):
            return ctx.enter_context(nc.semaphore(name))

        ident = sb("ident", [P, P])
        p_int = sb("p_int", [P, 1], I32)
        chan_int = sb("chan_int", [P, 1], I32)
        par_int = sb("par_int", [P, 1], I32)
        quad_int = sb("quad_int", [P, 1], I32)
        low_half = sb("low_half", [P, 1])
        quad_of_p = sb("quad_of_p", [P, 1])
        chan_of_p = sb("chan_of_p", [P, 1])
        parity = sb("parity", [P, 2])
        p_col = sb("p_col", [P, 1])
        step_of = sb("step_of", [P, KC])
        rstep_of = sb("rstep_of", [P, KC])
        ramp = sb("ramp", [P, NE])
        sc_w = sb("sc_w", [P, 2 * NG], I32)
        row_w = sb("row_w", [P, NG], I32)
        cmask = sb("cmask", [P, NG])
        quad_iota = sb("quad_iota", [P, BPG])
        quad_hot = sb("quad_hot", [P, BPG])
        cmask4 = sb("cmask4", [P, NG, BPG])
        w_raw = sb("w_raw", [P, NG, HID])
        w_bd = sb("w_bd", [P, NG // 2, BPG, HID])
        sid_e = sb("sid_e", [NS, B], I32)
        onehot_e = sb("onehot_e", [NS, 2, B // 2])
        bs_sb = sb("bs_sb", [NS, HID])
        bias_h = sb("bias_h", [P, B // 2])
        w2_bd = sb("w2_bd", [P, 2 * C])
        b2_col = sb("b2_col", [P, 1])
        c_t = sb("c_t", [P, 2, T])
        seq_sb = sb("seq_sb", [P, B], I32)
        tmask = sb("tmask", [P, KC, B])
        clen_sb = sb("clen_sb", [P, B], I32)
        lmask = sb("lmask", [P, KC, B])
        wb_hi = sb("wb_hi", [P, KC, T], F16)
        wb_lo = sb("wb_lo", [P, KC, T], BF16)
        ar_hi = sb("ar_hi", [P, KC, LR], F16)
        ar_lo = sb("ar_lo", [P, KC, LR], BF16)
        b_hi = sb("b_hi", [P, T], F16)
        b_lo = sb("b_lo", [P, T], BF16)
        bb_col = sb("bb_col", [P, KC])
        up_st = sb("up_st", [P, NH, M], F16)
        down_sb = sb("down_sb", [P, NH, DH])
        perm_sb = sb("perm_sb", [P, KC], I32)
        permh_sb = sb("permh_sb", [P, NH // 2], I32)
        yrow_sb = sb("yrow_sb", [P, NH // 2], I32)
        lo_rows = sb("lo_rows", [P, 1])
        orow_sb = sb("orow_sb", [P, NA, HQ], I32)
        x_sb = sb("x_sb", [P, NG, T])
        def x_part(n, part):
            t = x_sb[:, n - NG // 2, :].bitcast((F16, BF16)[part])
            return t[:, T * part:T * (part + 1)]

        def w_part(n, part):
            t = w_bd[:, n - NG // 2].rearrange("p b h -> p (b h)").bitcast((F16, BF16)[part])
            return t[:, BPG * HID * part:BPG * HID * (part + 1)]

        def raw_part(part):
            t = w_raw[:, 0:NG // 2, :].rearrange("p n h -> p (n h)").bitcast((F16, BF16)[part])
            return t[:, NG // 2 * HID * part:NG // 2 * HID * (part + 1)].rearrange("p (n h) -> p n h", h=HID)

        hid0 = sb("hid0", [P, 8, T])
        c0 = hid0[:, 4:8, :]
        c0_hi = sb("c0_hi", [P, 2, KC, TOK], F16)
        c0_lo = sb("c0_lo", [P, 2, KC, TOK], BF16)
        lg = sb("lg", [P, GPT, NE])
        rt = sb("rt", [P, 6, GPT, NE])
        rs = sb("rs", [P, 8, GPT])
        re_ = sb("re_", [P, 5, GPT])
        re_i = sb("re_i", [P, GPT], I32)
        hw = sb("hw", [P, GPT, P])
        hwt_hi = sb("hwt_hi", [P, TOK], F16)
        hwt_lo = sb("hwt_lo", [P, TOK], BF16)
        u = sb("u", [P, 2, KC, C, BPT])
        u_hi = sb("u_hi", [P, KC, C, B], F16)
        u_lo = sb("u_lo", [P, KC, C, B], BF16)
        toep_0 = sb("toep_0", [P, 8, 2, T], F16)
        spare = toep_0[:, :, :, :].rearrange("p n two t -> p (n two t)").bitcast(F32)
        wb_t = spare[:, 0:KC * T].rearrange("p (k t) -> p k t", k=KC)
        up_t = spare[:, KC * T:KC * T + NH * M].rearrange("p (h m) -> p h m", h=NH)
        spare = u_lo[:, :, :, :].rearrange("p k c b -> p (k c b)").bitcast(F32)
        ar_t = spare[:, 0:KC * LR].rearrange("p (k n) -> p k n", k=KC)
        b_t = spare[:, KC * LR:KC * LR + T]
        kz = sb("kz", [C, NST + 1])
        ke = sb("ke", [C, NST + 1])
        ksc = sb("ksc", [C, NST + 1], I32)
        k4t = sb("k4t", [P, 4, C])
        lgrid = sb("lgrid", [P, NJ + NI])
        offs = sb("offs", [P, 4])
        halves = sb("halves", [P, 2])
        ph = sb("ph", [P, C, NL])
        turns = sb("turns", [P, C, NL])
        spare = turns[0:C].rearrange("p h l -> p (h l)")
        ks = spare[:, 0:15 * (NST + 1)].rearrange("p (n s) -> p n s", n=15)
        k4 = spare[:, 1024:1024 + 8 * NST].rearrange("p (a c n) -> p a c n", a=4, c=2)
        kc = spare[:, 1536:1536 + 2 * NST].rearrange("p (n two) -> p n two", two=2)
        kai = spare[:, 1664:1664 + NST]
        ksin = spare[:, 1728:1728 + 2 * NST].rearrange("p (two n) -> p two n", two=2)
        tables = sb("tables", [P, 2 * C * B])
        decay = tables[:, 0:C * (NJ + NI)].rearrange("p (h j) -> p h j", h=C)
        FINE, COARSE = C * (NJ + NI), C * (2 * NJ + NI)
        fine = tables[:, FINE:COARSE].rearrange("p (h j) -> p h j", h=C)
        coarse = tables[:, COARSE:COARSE + C * NI].rearrange("p (h j) -> p h j", h=C)
        coarse2 = tables[:, COARSE + C * NI:COARSE + 2 * C * NI].rearrange("p (h j) -> p h j", h=C)
        d_bc = sb("d_bc", [NI, C])
        last_p = sb("last_p", [NI, 1])
        k_sb = ph[0:NI, 0:C // 2, :].rearrange("p h l -> p (h l)").rearrange("p (h j) -> p h j", j=NJ)
        k_half = ph[0:NI, C // 2:C, :].rearrange("p h l -> p (h l)").bitcast(F16).rearrange(
            "p (two h j) -> p h two j", two=2, j=NJ)
        zeros = sb("zeros", [C, 2, P], F16)
        def toep(h, part):
            if h < C // 4:
                t = toep_0[:, h]
            elif h < C // 2:
                t = (ph, turns)[h // 4 - 2].rearrange("p h l -> p (h l)").bitcast(F16)
                t = t.rearrange("p (n two l) -> p n two l", two=2, l=T)[:, h % 4]
            else:
                t = x_sb[:, h - C // 2, :].bitcast(F16).rearrange("p (two l) -> p two l", two=2)
            return t if part is None else t[:, part, :] if part == 0 else t[:, part, :].bitcast(BF16)

        y32 = w_raw[:, :, :].rearrange("p n h -> p (n h)").rearrange("p (n c k b) -> p n c k b", n=2, c=2, k=KC)

        def y_part(quarter, part):
            if quarter % 2 == 1:
                return c0_lo[:, part].bitcast(F16)
            t = w_bd[:, :, :, :].rearrange("p n b h -> p (n b h)").bitcast(F16)
            return t.rearrange("p (two k n) -> p two k n", two=2, k=KC)[:, part]

        def y_pair(n, part):
            j = n % (CPQ // 2)
            return y_part(n // (CPQ // 2), part)[:, :, 2 * B * j:2 * B * (j + 1)].rearrange("p k (c b) -> p c k b", c=2)

        def stacked(a, h):
            if a == 0:
                return toep(h, None).rearrange("p two l -> p (two l)")
            t = (w_bd[:, :, :, :].rearrange("p n b h -> p (n b h)"), None, tables[:, 0:2048], tables[:, 2048:4096])[h // 4]
            if h // 4 == 1:
                t = (wb_hi, wb_lo)[h % 4 // 2].rearrange("p k t -> p (k t)").bitcast(F16)
                return t[:, TOKA * (h % 2):TOKA * (h % 2 + 1)]
            return t.bitcast(F16)[:, TOKA * (h % 4):TOKA * (h % 4 + 1)]

        hid1 = hid0
        ot = u[:, :, :, :, :].rearrange("p a k h b -> p (a k h b)").rearrange("p (n t) -> p n t", t=TOKA)
        duo = [ctx.enter_context(nc.psum_tensor(f"duo{i}", [P, 2, 512], F32)) for i in range(4)]
        bank = [duo[i // 2][:, i % 2, :] for i in range(8)]
        ps_h = bank[0:3]
        ps_g = bank[3]
        ps_c = bank[4:6]
        ps_f = bank[6:8]
        ps_y = bank[0:2]
        ps_u = (duo[1], duo[2], duo[0])
        ps_o = bank[6:8]

        s_idx = sem("s_idx")
        s_seq = sem("s_seq")
        s_clen = sem("s_clen")
        s_b2 = sem("s_b2")
        s_ct = sem("s_ct")
        s_tu = sem("s_tu")
        s_r0 = sem("s_r0")
        s_g0 = sem("s_g0")
        s_k4p = sem("s_k4p")
        s_bs = sem("s_bs")
        s_w2 = sem("s_w2")
        s_x = [sem(f"s_x{i}") for i in range(NG)]
        s_wb = sem("s_wb")
        s_ar = sem("s_ar")
        s_bb = sem("s_bb")
        s_kin = sem("s_kin")
        s_l1 = sem("s_l1")
        s_upd = sem("s_upd")
        s_dbc = sem("s_dbc")
        s_cst = sem("s_cst")
        s_idn = sem("s_idn")
        s_z0 = sem("s_z0")
        s_row = sem("s_row")
        s_wg = [sem(f"s_wg{i}") for i in range(NG)]
        s_wbd = sem("s_wbd")
        s_xh = sem("s_xh")
        s_xl = sem("s_xl")
        s_ohe = sem("s_ohe")
        s_yrow = sem("s_yrow")
        s_hd = sem("s_hd")
        s_hg = sem("s_hg")
        s_hu = sem("s_hu")
        s_cv = sem("s_cv")
        s_ch = sem("s_ch")
        s_cl = sem("s_cl")
        s_wh = sem("s_wh")
        s_wl = sem("s_wl")
        s_up = sem("s_up")
        s_ul = sem("s_ul")
        s_fd = [sem(f"s_fd{i}") for i in range(2)]
        s_ff = [sem(f"s_ff{i}") for i in range(2)]
        s_hwt = sem("s_hwt")
        s_ka = sem("s_ka")
        s_kb = sem("s_kb")
        s_ke = sem("s_ke")
        s_pch = sem("s_pch")
        s_kf = sem("s_kf")
        s_kt0 = sem("s_kt0")
        s_kd0 = sem("s_kd0")
        s_wbl = sem("s_wbl")
        s_k4 = sem("s_k4")
        s_kt = sem("s_kt")
        s_kc = sem("s_kc")
        s_ksk = sem("s_ksk")
        s_khi = sem("s_khi")
        s_ks = sem("s_ks")
        s_kr = sem("s_kr")
        s_tp = [sem(f"s_tp{i}") for i in range(C // 4)]
        s_xt = [sem(f"s_xt{g}") for g in range(NT)]
        s_uf = sem("s_uf")
        s_yh = sem("s_yh")
        s_cd = sem("s_cd")
        s_yf = sem("s_yf")
        s_ye = sem("s_ye")
        s_ys = [sem(f"s_ys{g}") for g in range(4)]
        s_yg = [sem(f"s_yg{i}") for i in range(NA * NH // 2)]
        s_ud = sem("s_ud")
        s_ug = sem("s_ug")
        s_s2 = sem("s_s2")
        s_st = sem("s_st")
        s_od = sem("s_od")
        s_oe = sem("s_oe")
        s_res = [sem(f"s_res{g}") for g in range(NT)]
        s_add = [sem(f"s_add{g}") for g in range(4)]
        s_lr3 = sem("s_lr3")
        s_hw3 = sem("s_hw3")
        s_kd = sem("s_kd")
        s_dch = sem("s_dch")

        names = ["bias"]
        for g in range(NT):
            names += ([f"lr{g}0", f"lr{g}1"] if g < NT - 1 else []) + [f"hw{g}"]
            names += [f"oc{g}{i}" for i in range(1, KC)]
        unit = {n: i for i, n in enumerate(names)}

        def ring(n):
            return ps_f[unit[n] % 2]

        def linear_bank(g, i):
            return ps_g if i == 0 else ring(f"oc{g}{i}")

        def wait_filled(eng, n):
            eng.wait_ge(s_fd[unit[n] % 2], unit[n] // 2 + 1)

        def wait_freed(eng, n):
            eng.wait_ge(s_ff[unit[n] % 2], unit[n] // 2 + 1)

        def wait_free(eng, n):
            if unit[n] >= 2:
                eng.wait_ge(s_ff[unit[n] % 2], unit[n] // 2)

        def filled(ins, n):
            ins.then_inc(s_fd[unit[n] % 2], 1)

        def freed(ins, n):
            ins.then_inc(s_ff[unit[n] % 2], 1)

        sess_row = sess_id.rearrange("(one b) -> one b", one=1)

        regions = ((slice(0, NJ), offs[:, 2:3], offs[:, 3:4]), (slice(NJ, NJ + NI), -PI_BELOW, PI_BELOW))
        phase, whole = ph[:, :, 0:NJ + NI], turns[:, :, 0:NJ + NI]
        re, im = k4[:, 0, 0, :], k4[:, 1, 0, :]
        em1, ex, exm2 = ks[:, 6, 0:NST], ks[:, 7, 0:NST], ks[:, 3, 0:NST]
        er, ei = ks[:, 8, 0:NST], ks[:, 9, 0:NST]
        nr, ni, t1 = ks[:, 10, 0:NST], ks[:, 11, 0:NST], ks[:, 12, 0:NST]
        ar, ai, inv = ks[:, 13, 0:NST], kai[:, :], ks[:, 14, 0:NST]

        block = ctx.enter_context(nc.Block())

        @block.sync
        def _(sp):
            sp.dma_start(sc_w[:, :], bass.AP(tensor=sess_chan_by4.tensor, offset=0, ap=[[2 * NG, BPG], [0, C], [1, 2 * NG]])
                         ).then_inc(s_idx, 16)
            xg = x.rearrange("(g b) c t -> g (b c) t", b=BPG)
            for i in range(GPT):
                sp.dma_start(x_sb[:, i, :], xg[i]).then_inc(s_x[i], 16)
            sp.dma_start(seq_sb[:, :], seq_len.rearrange("(one b) -> one b", one=1).broadcast_to([P, B])).then_inc(s_seq, 16)
            sp.dma_start(ar_t, low_router_t.rearrange("(k p) n -> p k n", p=P)).then_inc(s_ar, 16)
            sp.dma_start(kz[:, 0:NST], log_a_re).then_inc(s_kin, 16)
            sp.dma_start(kz[:, NST:NST + 1], log_dt.rearrange("(h one) -> h one", one=1)).then_inc(s_kin, 16)
            sp.dma_start(kai[:, :], a_im).then_inc(s_kin, 16)
            sp.dma_start(kc[:, :, :], c_ri).then_inc(s_kin, 16)
            for i in range(GPT, 2 * GPT):
                sp.dma_start(x_sb[:, i, :], xg[i]).then_inc(s_x[i], 16)
            sp.dma_start(wb_t, w_base_t.rearrange("(k p) o -> p k o", p=P)).then_inc(s_wb, 16)
            sp.dma_start(b_t, lora_b_t).then_inc(s_wb, 16)
            sp.dma_start(bb_col[:, :], b_base_c).then_inc(s_bb, 16)
            sp.dma_start(clen_sb[:, :], conv_len.rearrange("(one b) -> one b", one=1).broadcast_to([P, B])).then_inc(s_clen, 16)
            sp.dma_start(perm_sb[:, :], perm_c).then_inc(s_l1, 16)
            for r in range(4):
                sp.dma_start(permh_sb[DH * r:DH * (r + 1), :], perm_h[r // 2]).then_inc(s_l1, 16)
            sp.dma_start(d_bc[:, :], d_skip.rearrange("(one h) -> one h", one=1).broadcast_to([NI, C])).then_inc(s_dbc, 16)

            def load_steps(g):
                if g >= 2:
                    sp.wait_ge(s_res[g - 2], 32)
                    sp.wait_ge(s_ul, KC * (g - 1))
                sp.dma_start(u[:, g % 2].rearrange("p k h b -> p k (h b)"),
                             x_steps[g].rearrange("(k p) h b -> p k (h b)", p=P)).then_inc(s_xt[g], 16)

            def store_result(g):
                for i in (KC - 2, KC - 1):
                    wait_freed(sp, f"oc{g}{i}")
                for a in range(NA):
                    sp.dma_start(out[a, :, g].rearrange("(k p) h b -> p k (h b)", p=P),
                                 u[:, g % 2, :, CPA * a:CPA * (a + 1), :].rearrange("p k h b -> p k (h b)")).then_inc(s_res[g], 16)

            load_steps(0)
            for i in range(2 * GPT, 3 * GPT):
                sp.dma_start(x_sb[:, i, :], xg[i]).then_inc(s_x[i], 16)
            load_steps(1)
            for i in range(3 * GPT, NG):
                sp.dma_start(x_sb[:, i, :], xg[i]).then_inc(s_x[i], 16)
            for r in range(4):
                sp.dma_start(up_t[DH * r:DH * (r + 1)], up.rearrange("h d m -> d h m")).then_inc(s_upd, 16)
            sp.dma_start(down_sb[:, :, :], down.rearrange("h m d -> m h d")).then_inc(s_l1, 16)
            store_result(0)
            load_steps(2)
            store_result(1)
            load_steps(3)
            sp.dma_start(k_rev[:, :, T:KLEN], zeros[:, :, :]).then_inc(s_kr, 16)
            sp.wait_ge(s_ks, 1)
            for part in range(2):
                sp.dma_start(k_rev[:, part, 0:T].rearrange("h (i j) -> i h j", j=NJ), k_half[:, :, part, :]).then_inc(s_kr, 16)
            sp.wait_ge(s_kr, 48)

            def load_toeplitz(g):
                for h in range(CPQ * g, CPQ * (g + 1)):
                    src = bass.AP(tensor=k_rev, offset=2 * h * KLEN, ap=[[1, P], [KLEN, 2], [1, T]])
                    sp.dma_start(toep(h, None), src).then_inc(s_tp[h // 4], 16)

            def store_rows(g):
                sp.wait_ge(s_ye, (g + 1) * CPQ // 2)
                for part in range(2):
                    sp.dma_start(y_rows[g // 2][T * part:T * (part + 1), TOK * (g % 2):TOK * (g % 2 + 1)].rearrange(
                        "(k p) n -> p k n", p=P), y_part(g, part)).then_inc(s_ys[g], 16)

            sp.wait_ge(s_wbl, 1)
            sp.wait_ge(s_up, 2)
            load_toeplitz(0)
            load_toeplitz(1)
            store_result(2)
            sp.wait_ge(s_hd, 2 * NG)
            load_toeplitz(2)
            load_toeplitz(3)
            store_rows(0)
            store_rows(1)
            store_result(3)
            store_rows(2)
            store_rows(3)

        @block.gpsimd
        def _(pool):
            nc.gpsimd.memset(w2_bd[:, :], 0.0)
            nc.gpsimd.memset(zeros[:, :, :], 0.0).then_inc(s_z0, 1)
            for i, v in enumerate((HALF_PI, 0.0)):
                nc.gpsimd.memset(halves[:, i:i + 1], v)
            nc.gpsimd.iota(p_int[:, :], [[0, 1]], base=0, channel_multiplier=1)
            nc.gpsimd.iota(p_col[:, :], [[0, 1]], base=0, channel_multiplier=1, allow_small_or_imprecise_dtypes=True)
            nc.gpsimd.iota(step_of[:, :], [[P, KC]], base=0, channel_multiplier=1, allow_small_or_imprecise_dtypes=True)
            nc.gpsimd.iota(rstep_of[:, :], [[P, KC]], base=P - 1, channel_multiplier=-1, allow_small_or_imprecise_dtypes=True)
            nc.gpsimd.iota(quad_iota[:, :], [[1, BPG]], base=0, channel_multiplier=0, allow_small_or_imprecise_dtypes=True)
            nc.gpsimd.iota(ramp[:, :], [[-1, NE]], base=NE, channel_multiplier=0, allow_small_or_imprecise_dtypes=True)
            nc.gpsimd.iota(lgrid[:, 0:NJ], [[-1, NJ]], base=NJ - 1, channel_multiplier=0, allow_small_or_imprecise_dtypes=True)
            nc.gpsimd.iota(lgrid[:, NJ:NJ + NI], [[-NJ, NI]], base=T - NJ, channel_multiplier=0,
                           allow_small_or_imprecise_dtypes=True).then_inc(s_cst, 1)
            nc.gpsimd.memset(ident[:, :], 0.0).then_inc(s_idn, 1)
            pool.wait_ge(s_idn, 1)
            nc.gpsimd.affine_select(out=ident[:, :], in_=ident[:, :], compare_op=ALU.not_equal, fill=1.0, base=0,
                                    pattern=[[-1, P]], channel_multiplier=1).then_inc(s_idn, 1)
            nc.gpsimd.memset(low_half[:, :], 1.0).then_inc(s_idn, 1)
            pool.wait_ge(s_idn, 3)
            nc.gpsimd.affine_select(out=low_half[:, :], in_=low_half[:, :], compare_op=ALU.is_ge, fill=0.0, base=-P // 2,
                                    pattern=[[0, 1]], channel_multiplier=1).then_inc(s_idn, 1)
            pool.wait_ge(s_row, 1)

            def session_weights(i):
                nc.gpsimd.indirect_dma_start(
                    out=w_raw[:, i, :], out_offset=None, in_=w_sess.rearrange("e c h -> (e c) h"),
                    in_offset=bass.IndirectOffsetOnAxis(ap=row_w[:, i:i + 1], axis=0)).then_inc(s_wg[i], 16)

            for i in range(NG):
                session_weights(i)

            def stack_up():
                pool.wait_ge(s_up, 1)
                nc.gpsimd.tensor_tensor(up_st[:, :, :], up_t, up_st[:, :, :], ALU.subtract).then_inc(s_up, 1)

            pool_chain = [0]

            def then(ins):
                pool_chain[0] += 1
                ins.then_inc(s_pch, 1)
                pool.wait_ge(s_pch, pool_chain[0])

            def kernel_gain():
                G = nc.gpsimd
                pool.wait_ge(s_kb, 1)
                pool.wait_ge(s_ke, 1)
                cr, ci = kc[:, :, 0], kc[:, :, 1]
                then(G.tensor_tensor(ei, ex, ksin[:, 0, :], ALU.mult))
                then(G.tensor_tensor(er, ksin[:, 1, :], ksin[:, 1, :], ALU.mult))
                then(G.tensor_tensor(er, er, exm2, ALU.mult))
                then(G.tensor_tensor(er, er, em1, ALU.add))
                then(G.tensor_tensor(nr, cr, er, ALU.mult))
                then(G.tensor_tensor(t1, ci, ei, ALU.mult))
                then(G.tensor_tensor(nr, nr, t1, ALU.subtract))
                then(G.tensor_tensor(ni, cr, ei, ALU.mult))
                then(G.tensor_tensor(t1, ci, er, ALU.mult))
                then(G.tensor_tensor(ni, ni, t1, ALU.add))
                then(G.tensor_tensor(t1, nr, ar, ALU.mult))
                then(G.tensor_tensor(er, ni, ai, ALU.mult))
                then(G.tensor_tensor(t1, t1, er, ALU.add))
                then(G.tensor_tensor(ei, nr, ai, ALU.mult))
                then(G.tensor_tensor(er, ni, ar, ALU.mult))
                then(G.tensor_tensor(ei, ei, er, ALU.subtract))
                then(G.tensor_tensor(k4[:, 2, 0, :], t1, inv, ALU.mult))
                then(G.tensor_tensor(k4[:, 2, 1, :], ei, inv, ALU.mult))
                G.tensor_copy(k4[:, 3, 0, :], k4[:, 2, 1, :])
                G.tensor_scalar(k4[:, 3, 1, :], k4[:, 2, 0, :], -1.0, None, ALU.mult).then_inc(s_k4, 1)

            def cond_lo(n):
                g, i = n // GPT, n % GPT
                pool.wait_ge(s_ch, n + 1)
                nc.gpsimd.tensor_tensor(c0_lo[:, g % 2, :, P * i:P * (i + 1)], c0[:, n % 4, :].rearrange("p (k n) -> p k n", k=KC),
                                        c0_hi[:, g % 2, :, P * i:P * (i + 1)], ALU.subtract).then_inc(s_cl, 1)

            def result_lo(g, i):
                pool.wait_ge(s_uf, KC * g + i + 1)
                b = slice(BPT * g, BPT * (g + 1))
                nc.gpsimd.tensor_tensor(u_lo[:, i, :, b], u[:, g % 2, i], u_hi[:, i, :, b], ALU.subtract).then_inc(s_ul, 1)

            for g in range(NT):
                for i in range(GPT):
                    cond_lo(GPT * g + i)
                if g == 0:
                    pool.wait_ge(s_wh, 2)
                    nc.gpsimd.tensor_tensor(wb_lo[:, :, :], wb_t, wb_hi[:, :, :], ALU.subtract).then_inc(s_wbl, 1)
                    kernel_gain()
                if g == 1:
                    for n in range(SPLIT, NG):
                        pool.wait_ge(s_xh, n - SPLIT + 1)
                        nc.gpsimd.tensor_tensor(x_part(n, 1), x_sb[:, n, :], x_part(n, 0), ALU.subtract).then_inc(s_xl, 1)
                    pool.wait_ge(s_kf, 1)
                    nc.gpsimd.tensor_tensor(decay, k4t[:, 0, :].unsqueeze(2).broadcast_to([P, C, NJ + NI]),
                                            lgrid[:, 0:NJ + NI].unsqueeze(1).broadcast_to([P, C, NJ + NI]), ALU.mult).then_inc(s_kd0, 1)
                if g == NT - 1:
                    pool.wait_ge(s_khi, 1)
                    nc.gpsimd.tensor_tensor(k_half[:, :, 1, :].bitcast(BF16), k_sb, k_half[:, :, 0, :], ALU.subtract).then_inc(s_ks, 1)
                if g >= 1:
                    for i in range(KC):
                        result_lo(g - 1, i)
                if g == 2:
                    stack_up()
            for i in range(KC):
                result_lo(NT - 1, i)

            pool.wait_ge(s_yrow, 1)
            for a in range(NA):
                for q in range(2):
                    pool.wait_ge(s_ys[2 * a + q], 32)
                for j in range(NH // 2):
                    nc.gpsimd.indirect_dma_start(
                        out=stacked(a, 2 * j), out_offset=None, in_=y_rows[a][:, :],
                        in_offset=bass.IndirectOffsetOnAxis(ap=yrow_sb[:, j:j + 1], axis=0)).then_inc(s_yg[NH // 2 * a + j], 16)
            for g in range(NT):
                pool.wait_ge(s_res[g], 32)
            for n in range(NA * HQ):
                pool.wait_ge(s_oe, 2 * (n + 1))
                nc.gpsimd.indirect_dma_start(
                    out=out_rows, out_offset=bass.IndirectOffsetOnAxis(ap=orow_sb[:, n // HQ, n % HQ:n % HQ + 1], axis=0),
                    in_=ot[:, n % 4, :], in_offset=None, compute_op=ALU.add).then_inc(s_add[n % 4], 16)
            for i in range(4):
                pool.wait_ge(s_add[i], 16 * NA * HQ // 4)

        @block.scalar
        def _(act):
            act.dma_start(sid_e[:, :], sess_row.broadcast_to([NS, B])).then_inc(s_bs, 16)
            act.dma_start(bs_sb[:, :], b_sess).then_inc(s_bs, 16)
            act.dma_start(b2_col[:, :], bass.AP(tensor=b2.tensor, offset=0, ap=[[0, BPG], [1, C], [1, 1]])).then_inc(s_b2, 16)
            act.wait_ge(s_z0, 1)
            for i in range(2):
                act.dma_start(w2_bd[HID * i:HID * (i + 1), C * i:C * (i + 1)], w2).then_inc(s_w2, 16)

            def cond_bias(n):
                if n == 0:
                    act.wait_ge(s_b2, 16)
                act.wait_ge(s_hu, n + 1)
                if n >= 2:
                    act.wait_ge(s_tu, n - 1)
                nc.scalar.activation(c_t[:, n % 2, :], ps_g[:, :], ACT.Identity, bias=b2_col[:, 0:1]).then_inc(s_ct, 1)

            def gelus(g):
                for n in range(GPT * g, GPT * (g + 1)):
                    for m in (2 * n, 2 * n + 1):
                        act.wait_ge(s_hd, m + 1)
                        if m >= 4:
                            act.wait_ge(s_hu, m // 2 - 1)
                        nc.scalar.activation(hid0[:, m % 4, :], ps_h[m % 3][:, :], ACT.Gelu,
                                             bias=bias_h[:, m:m + 1]).then_inc(s_hg, 1)
                    if n > GPT * g:
                        cond_bias(n - 1)
                cond_bias(n)

            act.wait_ge(s_ff[unit["bias"] % 2], 1)
            def cond_hi(n):
                g, i = n // GPT, n % GPT
                act.wait_ge(s_cv, n + 1)
                if g >= 2 and i == 0:
                    wait_filled(act, f"oc{g - 2}{KC - 1}")
                nc.scalar.copy(c0_hi[:, g % 2, :, P * i:P * (i + 1)],
                               c0[:, n % 4, :].rearrange("p (k n) -> p k n", k=KC)).then_inc(s_ch, 1)

            gelus(0)
            act.wait_ge(s_ar, 16)
            nc.scalar.copy(ar_hi[:, :, :], ar_t).then_inc(s_wh, 1)
            for n in range(GPT):
                cond_hi(n)
            act.wait_ge(s_wb, 32)
            nc.scalar.copy(wb_hi[:, :, :], wb_t).then_inc(s_wh, 1)
            nc.scalar.copy(b_hi[:, :], b_t).then_inc(s_wh, 1)
            act.wait_ge(s_ka, 1)
            nc.scalar.activation(ksin[:, 0, :], ks[:, 5, 0:NST], ACT.Sin)
            nc.scalar.activation(ksin[:, 1, :], ks[:, 5, 0:NST], ACT.Sin, scale=0.5).then_inc(s_kb, 1)
            for g in range(NT):
                if g + 1 < NT:
                    gelus(g + 1)
                    for n in range(GPT * (g + 1), GPT * (g + 2) - (g < NT - 2)):
                        cond_hi(n)
                wait_filled(act, f"hw{g}")
                if g >= 1:
                    wait_filled(act, f"oc{g - 1}{KC - 1}")
                nc.scalar.copy(hwt_hi[:, :], ring(f"hw{g}")[:, :]).then_inc(s_hwt, 1)
                if g == 0:
                    act.wait_ge(s_kf, 1)
                    for cols, bias in ((slice(0, NJ), offs[:, 0:1]), (slice(NJ, NJ + NI), halves[:, 1:2])):
                        last = nc.scalar.activation(turns[:, :, cols], ph[:, :, cols], ACT.Identity, bias=bias, scale=1.0 / (4 * HALF_PI))
                    last.then_inc(s_kt0, 1)
                if g == 1:
                    act.wait_ge(s_ka, 2)
                    act.wait_ge(s_kd0, 1)
                    for cols, bias, sign in ((slice(0, NJ), offs[:, 1:2], 1.0), (slice(NJ, NJ + NI), halves[:, 1:2], 1.0),
                                             (slice(NJ + NI, NL), halves[:, 0:1], -1.0)):
                        nc.scalar.activation(turns[:, :, cols], ph[:, :, cols], ACT.Sin, bias=bias, scale=sign)
                    nc.scalar.activation(decay, decay, ACT.Exp).then_inc(s_kb, 1)
                    act.wait_ge(s_upd, 64)
                    act.wait_ge(s_idn, 4)
                    nc.scalar.activation(up_st[:, :, :], up_t, ACT.Identity, scale=low_half[:, 0:1]).then_inc(s_up, 1)
                for i in range(KC):
                    if i == 0:
                        act.wait_ge(s_g0, g + 1)
                    else:
                        wait_freed(act, f"oc{g}{i}")
                    nc.scalar.copy(u_hi[:, i, :, BPT * g:BPT * (g + 1)], u[:, g % 2, i]).then_inc(s_uf, 1)
                    if g == NT - 2 and i == 0:
                        act.wait_ge(s_kd, 2)
                        for half in range(2):
                            last = nc.scalar.copy(k_sb[:, C // 2 * half:C // 2 * (half + 1), :],
                                                  ps_c[half][0:NI, :].rearrange("p (h j) -> p h j", j=NJ))
                        last.then_inc(s_kc, 1)
                    if g == NT - 2 and i == 1:
                        act.wait_ge(s_ksk, 1)
                        nc.scalar.copy(k_half[:, :, 0, :], k_sb).then_inc(s_khi, 1)
                    if i == 0 and g < NT - 2:
                        cond_hi(GPT * (g + 2) - 1)
                    if i == 0 and g == 0:
                        for n in range(SPLIT, NG):
                            act.wait_ge(s_x[n], 16)
                            act.wait_ge(s_hd, 2 * (n - NG // 2 + 1))
                            nc.scalar.copy(x_part(n, 0), x_sb[:, n, :]).then_inc(s_xh, 1)
            for n in range(C // 2):
                quarter, j = n // (CPQ // 2), n % (CPQ // 2)
                if quarter >= 2 and j == 0:
                    act.wait_ge(s_ys[quarter - 2], 32)
                act.wait_ge(s_yf, n + 1)
                nc.scalar.copy(y_pair(n, 0), y32[:, n % 2]).then_inc(s_yh, 1)
            for n in range(0, 4 * NH, 2):
                act.wait_ge(s_ud, n + 2)
                if n >= 8:
                    act.wait_ge(s_od, n // 4 - 1)
                nc.scalar.activation(hid1[:, n % 8:n % 8 + 2, :], ps_u[n // 2 % 3][:, :, :], ACT.Gelu).then_inc(s_ug, 2)

        @block.vector
        def _(dve):
            V = nc.vector
            chain = [0]

            def link(ins):
                chain[0] += 1
                ins.then_inc(s_dch, 1)
                dve.wait_ge(s_dch, chain[0])

            dve.wait_ge(s_cst, 1)
            link(V.tensor_scalar(chan_int[:, :], p_int[:, :], C - 1, None, ALU.bitwise_and))
            link(V.tensor_scalar(par_int[:, :], p_int[:, :], 5, 1, ALU.logical_shift_right, ALU.bitwise_and))
            link(V.tensor_copy(chan_of_p[:, :], chan_int[:, :]))
            link(V.tensor_copy(parity[:, 1:2], par_int[:, :]))
            dve.wait_ge(s_idx, 16)
            V.tensor_scalar(row_w[:, :], sc_w[:, 0:NG], float(C), chan_of_p[:, 0:1], ALU.mult, ALU.add).then_inc(s_row, 1)
            link(V.tensor_scalar(lo_rows[:, :], parity[:, 1:2], float(T), None, ALU.mult))
            link(V.tensor_scalar(quad_int[:, :], p_int[:, :], 5, None, ALU.logical_shift_right))
            link(V.tensor_copy(quad_of_p[:, :], quad_int[:, :]))
            link(V.tensor_scalar(quad_hot[:, :], quad_iota[:, :], quad_of_p[:, 0:1], None, ALU.is_equal))
            link(V.tensor_scalar(cmask[:, :], sc_w[:, NG:2 * NG], chan_of_p[:, 0:1], None, ALU.is_gt))
            link(V.tensor_tensor(cmask4[:, :, :], cmask[:, :].unsqueeze(2).broadcast_to([P, NG, BPG]),
                                 quad_hot[:, :].unsqueeze(1).broadcast_to([P, NG, BPG]), ALU.mult))
            dve.wait_ge(s_bs, 32)
            V.tensor_scalar(onehot_e[:, :, :], sid_e[:, :].rearrange("e (b two) -> e two b", two=2), p_col[0:NS, 0:1], None,
                            ALU.is_equal).then_inc(s_ohe, 1)
            def exp_small(dst_p, dst_scale, z, tmp_k, tmp_r):
                link(V.tensor_scalar(tmp_k, z, LOG2E, ROUND, ALU.mult, ALU.add))
                link(V.tensor_scalar(tmp_k, tmp_k, ROUND, -126.0, ALU.subtract, ALU.max))
                link(V.scalar_tensor_tensor(tmp_r, tmp_k, -LN2_HI, z, ALU.mult, ALU.add))
                link(V.scalar_tensor_tensor(tmp_r, tmp_k, -LN2_LO, tmp_r, ALU.mult, ALU.add))
                V.tensor_scalar(dst_scale, tmp_k, 127.0, 2.0 ** 23, ALU.add, ALU.mult)
                link(V.tensor_scalar(dst_p, tmp_r, EXP_COEFFS[0], None, ALU.mult))
                for c in EXP_COEFFS[1:]:
                    link(V.scalar_tensor_tensor(dst_p, dst_p, c, tmp_r, ALU.add, ALU.mult))

            N1 = NST + 1

            def kernel_phases():
                dve.wait_ge(s_kin, 64)
                exp_small(ks[:, 2, 0:N1], ksc[:, 0:N1], kz[:, :], ks[:, 0, 0:N1], ks[:, 1, 0:N1])
                link(V.scalar_tensor_tensor(ke[:, :], ks[:, 2, 0:N1], 1.0, ksc[:, 0:N1].bitcast(F32), ALU.add, ALU.mult))
                dt = ke[:, NST:N1]
                link(V.tensor_scalar(re, ke[:, 0:NST], dt, -1.0, ALU.mult, ALU.mult))
                link(V.tensor_scalar(im, kai[:, :], dt, None, ALU.mult))
                link(V.tensor_scalar(ks[:, 4, 0:NST], im, 1.0 / (4 * HALF_PI), ROUND, ALU.mult, ALU.add))
                link(V.tensor_scalar(ks[:, 4, 0:NST], ks[:, 4, 0:NST], ROUND, None, ALU.subtract))
                src = im
                for part in TWO_PI_PARTS:
                    link(V.scalar_tensor_tensor(ks[:, 5, 0:NST], ks[:, 4, 0:NST], -part, src, ALU.mult, ALU.add))
                    src = ks[:, 5, 0:NST]
                V.tensor_scalar(ks[:, 5, 0:NST], src, -PI_BELOW, PI_BELOW, ALU.max, ALU.min).then_inc(s_ka, 1)

            def kernel_exp():
                link(V.tensor_scalar(kz[:, 0:NST], re, -87.0, None, ALU.max))
                exp_small(ks[:, 2, 0:NST], ksc[:, 0:NST], kz[:, 0:NST], ks[:, 0, 0:NST], ks[:, 1, 0:NST])
                scale = ksc[:, 0:NST].bitcast(F32)
                link(V.tensor_scalar(ks[:, 3, 0:NST], scale, 1.0, None, ALU.subtract))
                link(V.tensor_tensor(em1, ks[:, 2, 0:NST], scale, ALU.mult))
                link(V.tensor_tensor(em1, em1, ks[:, 3, 0:NST], ALU.add))
                link(V.tensor_scalar(ex, em1, 1.0, None, ALU.add))
                V.tensor_scalar(exm2, ex, -2.0, None, ALU.mult)
                V.tensor_copy(k4[:, 0, 1, :], re)
                V.tensor_copy(k4[:, 1, 1, :], im)
                link(V.tensor_scalar(ar, ke[:, 0:NST], -1.0, None, ALU.mult))
                link(V.tensor_tensor(inv, ar, ar, ALU.mult))
                link(V.tensor_tensor(t1, ai, ai, ALU.mult))
                link(V.tensor_tensor(inv, inv, t1, ALU.add))
                link(V.tensor_scalar(inv, inv, 0.5, None, ALU.mult))
                V.reciprocal(inv, inv).then_inc(s_ke, 1)

            def weights(n):
                dve.wait_ge(s_wg[n], 16)
                if n >= NG // 2:
                    dve.wait_ge(s_hd, 2 * (n - NG // 2 + 1))
                m = cmask4[:, n, :].unsqueeze(2).broadcast_to([P, BPG, HID])
                if n < SPLIT:
                    V.tensor_tensor(w_bd[:, n % (NG // 2), :, :], w_raw[:, n, :].unsqueeze(1).broadcast_to([P, BPG, HID]),
                                    m, ALU.mult).then_inc(s_wbd, 1)
                else:
                    for part in range(2):
                        ins = V.tensor_tensor(w_part(n, part).rearrange("p (b h) -> p b h", h=HID),
                                              raw_part(part)[:, n - NG // 2, :].unsqueeze(1).broadcast_to([P, BPG, HID]), m, ALU.mult)
                    ins.then_inc(s_wbd, 1)

            def weights_parts():
                for n in range(SPLIT, NG):
                    dve.wait_ge(s_wg[n], 16)
                dve.wait_ge(s_wbd, SPLIT)
                link(V.tensor_copy(raw_part(0), w_raw[:, NG // 2:NG, :]))
                link(V.tensor_tensor(raw_part(1), w_raw[:, NG // 2:NG, :], raw_part(0), ALU.subtract))

            wait_filled(dve, "bias")
            ins = V.tensor_copy(bias_h[:, :], ring("bias")[:, 0:B // 2])
            freed(ins, "bias")
            def cond_out(n):
                g, i = n // GPT, n % GPT
                dve.wait_ge(s_tu, n + 1)
                if n >= 4:
                    dve.wait_ge(s_cl, n - 3)
                m = tmask[:, :, BPG * n:BPG * (n + 1)].unsqueeze(3).broadcast_to([P, KC, BPG, C])
                V.tensor_tensor(c0[:, n % 4, :].rearrange("p (k b s) -> p k b s", k=KC, s=C),
                                ps_c[n % 2][:, :].rearrange("p (k b s) -> p k b s", k=KC, s=C), m, ALU.mult).then_inc(s_cv, 1)

            def turned_lo(g):
                dve.wait_ge(s_hwt, g + 1)
                ins = V.tensor_tensor(hwt_lo[:, :], ring(f"hw{g}")[:, :], hwt_hi[:, :], ALU.subtract)
                freed(ins, f"hw{g}")

            def low_rank(g, i):
                return ps_h[i] if g == NT - 1 else ring(f"lr{g}{i}")

            def wide(a):
                return a.unsqueeze(2).broadcast_to([P, GPT, NE])

            ramps = ramp[:, :].unsqueeze(1).broadcast_to([P, GPT, NE])

            def top(logits, m, first, hot):
                link(V.tensor_reduce(rs[:, m, :], logits, AX_X, ALU.max))
                link(V.tensor_tensor(rt[:, 0], logits, wide(rs[:, m, :]), ALU.is_equal))
                link(V.tensor_tensor(rt[:, 0], rt[:, 0], ramps, ALU.mult))
                link(V.tensor_reduce(rs[:, first, :], rt[:, 0], AX_X, ALU.max))
                link(V.tensor_tensor(rt[:, hot], ramps, wide(rs[:, first, :]), ALU.is_equal))

            def route_top(g):
                for i in range(2):
                    if g == NT - 1:
                        dve.wait_ge(s_lr3, i + 1)
                    else:
                        wait_filled(dve, f"lr{g}{i}")
                    link(V.tensor_copy(lg[:, 2 * i:2 * i + 2, :],
                                       low_rank(g, i)[:, 0:2 * LR].rearrange("p (s n) -> p s n", n=LR)[:, :, P:LR]))
                top(lg[:, :, :], 0, 4, 1)
                link(V.scalar_tensor_tensor(rt[:, 2], rt[:, 1], -BIG, lg[:, :, :], ALU.mult, ALU.add))
                top(rt[:, 2], 1, 5, 3)

            def route_exp(g):
                link(V.tensor_tensor(rs[:, 2, :], rs[:, 1, :], rs[:, 0, :], ALU.subtract))
                link(V.tensor_scalar(rs[:, 2, :], rs[:, 2, :], -87.0, None, ALU.max))
                exp_small(re_[:, 2, :], re_i[:, :], rs[:, 2, :], re_[:, 0, :], re_[:, 1, :])
                link(V.scalar_tensor_tensor(rs[:, 3, :], re_[:, 2, :], 1.0, re_i[:, :].bitcast(F32), ALU.add, ALU.mult))

            def route_weights(g):
                link(V.tensor_scalar(rs[:, 6, :], rs[:, 3, :], 0.5, 0.5, ALU.mult, ALU.add))
                link(V.reciprocal(rs[:, 6, :], rs[:, 6, :]))
                link(V.tensor_tensor(rs[:, 7, :], rs[:, 6, :], rs[:, 3, :], ALU.mult))
                link(V.tensor_tensor(rt[:, 1], rt[:, 1], wide(rs[:, 6, :]), ALU.mult))
                link(V.tensor_tensor(rt[:, 3], rt[:, 3], wide(rs[:, 7, :]), ALU.mult))
                link(V.tensor_tensor(rt[:, 4], rt[:, 1], rt[:, 3], ALU.add))
                if g >= 1:
                    wait_filled(dve, f"hw{g - 1}")
                for i in range(2):
                    ins = V.tensor_tensor(
                        hw[:, 2 * i:2 * i + 2, :].rearrange("p s (e r) -> p s e r", e=NE),
                        low_rank(g, i)[:, 0:2 * LR].rearrange("p (s n) -> p s n", n=LR)[:, :, 0:P].rearrange("p s (e r) -> p s e r", e=NE),
                        rt[:, 4, 2 * i:2 * i + 2, :].unsqueeze(3).broadcast_to([P, 2, NE, RANK]), ALU.mult)
                    if g == NT - 1:
                        ins.then_inc(s_hw3, 1)
                    else:
                        freed(ins, f"lr{g}{i}")

            def kernel_tables():
                dve.wait_ge(s_k4p, 1)
                link(V.tensor_copy(k4t[:, :, :], ps_c[0][:, 0:4 * C].rearrange("p (a h) -> p a h", a=4)))
                V.tensor_tensor(phase, k4t[:, 1, :].unsqueeze(2).broadcast_to([P, C, NJ + NI]),
                                lgrid[:, :].unsqueeze(1).broadcast_to([P, C, NJ + NI]), ALU.mult).then_inc(s_kf, 1)

            def kernel_turns():
                dve.wait_ge(s_kt0, 1)
                link(V.tensor_scalar(whole, whole, ROUND, ROUND, ALU.add, ALU.subtract))

            def kernel_reduced(i):
                link(V.scalar_tensor_tensor(phase, whole, -TWO_PI_PARTS[i], phase, ALU.mult, ALU.add))

            def kernel_bounds():
                for cols, lo, hi in regions:
                    last = V.tensor_scalar(ph[:, :, cols], ph[:, :, cols], lo, hi, ALU.max, ALU.min)
                link(last)
                coarse_phase = ph[:, :, NJ:NJ + NI]
                V.scalar_tensor_tensor(ph[:, :, NJ + NI:NL], coarse_phase, -1.0, coarse_phase, ALU.mult, ALU.max).then_inc(s_ka, 1)

            def kernel_factors():
                dve.wait_ge(s_kb, 2)
                sines = turns
                link(V.tensor_tensor(coarse, sines[:, :, NJ + NI:NL],
                                     k4t[:, 2, :].unsqueeze(2).broadcast_to([P, C, NI]), ALU.mult))
                link(V.tensor_tensor(coarse2, sines[:, :, NJ:NJ + NI],
                                     k4t[:, 3, :].unsqueeze(2).broadcast_to([P, C, NI]), ALU.mult))
                link(V.tensor_tensor(coarse, coarse, coarse2, ALU.add))
                link(V.tensor_tensor(coarse, coarse, decay[:, :, NJ:NJ + NI], ALU.mult))
                V.tensor_tensor(fine, sines[:, :, 0:NJ], decay[:, :, 0:NJ], ALU.mult).then_inc(s_kt, 1)

            def kernel_skip():
                dve.wait_ge(s_kc, 1)
                V.tensor_tensor(k_sb[:, :, NJ - 1], k_sb[:, :, NJ - 1], d_bc[:, :], ALU.add).then_inc(s_ksk, 1)

            def result(g, i):
                if i == 0:
                    dve.wait_ge(s_xt[g], 16)
                if i == 0:
                    dve.wait_ge(s_r0, g + 1)
                else:
                    wait_filled(dve, f"oc{g}{i}")
                v = u[:, g % 2, i]
                ins = V.scalar_tensor_tensor(v, linear_bank(g, i)[:, :].rearrange("p (b s) -> p s b", s=C), bb_col[:, i:i + 1], v,
                                             ALU.add, ALU.add)
                if i == 0:
                    ins.then_inc(s_g0, 1)
                else:
                    freed(ins, f"oc{g}{i}")

            def set_rows():
                dve.wait_ge(s_dbc, 16)
                link(V.tensor_scalar(last_p[:, :], p_col[0:NI, :], float(NI - 1), None, ALU.is_equal))
                link(V.tensor_scalar(d_bc[:, :], d_bc[:, :], last_p[:, 0:1], None, ALU.mult))
                dve.wait_ge(s_l1, 96)
                link(V.tensor_scalar(permh_sb[:, :], permh_sb[:, :], P - 1, None, ALU.bitwise_xor))
                V.tensor_scalar(yrow_sb[:, :], permh_sb[:, :], lo_rows[:, 0:1], None, ALU.add)
                for a in range(NA):
                    last = V.tensor_scalar(orow_sb[:, a, :], perm_sb[:, :], float(T * a), None, ALU.add)
                last.then_inc(s_yrow, 1)

            for n in range(GPT + 1):
                weights(n)
            def offsets():
                for i, v in enumerate((0.25, HALF_PI)):
                    V.tensor_scalar(offs[:, i:i + 1], p_col[:, :], P / 2.0, v, ALU.is_lt, ALU.mult)
                link(V.tensor_scalar(offs[:, 2:4], p_col[:, :].broadcast_to([P, 2]), P / 2.0, -HALF_PI, ALU.is_lt, ALU.mult))
                V.tensor_scalar(offs[:, 2:3], offs[:, 2:3], -PI_BELOW, None, ALU.add)
                link(V.tensor_scalar(offs[:, 3:4], offs[:, 3:4], PI_BELOW, None, ALU.add))

            dve.wait_ge(s_seq, 16)
            link(V.tensor_tensor(tmask[:, :, :], step_of[:, :].unsqueeze(2).broadcast_to([P, KC, B]),
                                 seq_sb[:, :].unsqueeze(1).broadcast_to([P, KC, B]), ALU.is_lt))
            kernel_phases()
            offsets()
            for n in range(GPT):
                cond_out(n)
            dve.wait_ge(s_wh, 1)
            V.tensor_tensor(ar_lo[:, :, :], ar_t, ar_hi[:, :, :], ALU.subtract).then_inc(s_wl, 1)
            for n in range(GPT + 1, 2 * GPT):
                weights(n)
            kernel_exp()
            dve.wait_ge(s_clen, 16)
            V.tensor_tensor(lmask[:, :, :], rstep_of[:, :].unsqueeze(2).broadcast_to([P, KC, B]),
                            clen_sb[:, :].unsqueeze(1).broadcast_to([P, KC, B]), ALU.is_lt)
            dve.wait_ge(s_bb, 16)
            for g in range(NT - 1):
                if g + 2 < NT:
                    weights(GPT * (g + 2))
                route_top(g)
                cond_out(GPT * (g + 1))
                route_exp(g)
                cond_out(GPT * (g + 1) + 1)
                route_weights(g)
                cond_out(GPT * (g + 1) + 2)
                if g == 0:
                    dve.wait_ge(s_wh, 3)
                    V.tensor_tensor(b_lo[:, :], b_t, b_hi[:, :], ALU.subtract).then_inc(s_wl, 1)
                if g == NT - 2:
                    cond_out(NG - 1)
                turned_lo(g)
                if g == 0:
                    kernel_tables()
                if g + 2 < NT:
                    result(g, 0)
                    result(g, 1)
                    cond_out(GPT * (g + 1) + 3)
                    if g == 0:
                        weights_parts()
                    for n in range(GPT * (g + 2) + 1, GPT * (g + 3)):
                        weights(n)
                if g == 0:
                    kernel_turns()
                    result(g, 2)
                    kernel_reduced(0)
                    result(g, 3)
                    kernel_reduced(1)
                    kernel_reduced(2)
                    kernel_bounds()
                if g == 1:
                    set_rows()
                    result(g, 2)
                    result(g, 3)
                    kernel_factors()
            route_top(NT - 1)
            result(NT - 2, 0)
            result(NT - 2, 1)
            kernel_skip()
            route_exp(NT - 1)
            result(NT - 2, 2)
            route_weights(NT - 1)
            result(NT - 2, 3)
            turned_lo(NT - 1)
            for i in range(KC):
                result(NT - 1, i)

            def conv_out(n):
                dve.wait_ge(s_cd, 2 * (n + 1))
                if n >= 2:
                    dve.wait_ge(s_ye, n - 1)
                V.tensor_tensor(y32[:, n % 2], ps_y[n % 2][:, :].rearrange("p (c k b) -> p c k b", c=2, k=KC),
                                lmask[:, :, :].unsqueeze(1).broadcast_to([P, 2, KC, B]), ALU.mult).then_inc(s_yf, 1)

            def conv_lo(n):
                dve.wait_ge(s_yh, n + 1)
                V.tensor_tensor(y_pair(n, 1), y32[:, n % 2], y_pair(n, 0), ALU.subtract).then_inc(s_ye, 1)

            def both_halves(m):
                a, q = m // HQ, m % HQ
                for j in range(2 * q, 2 * q + 2):
                    dve.wait_ge(s_yg[NH // 2 * a + j], 16)
                    first, second = stacked(a, 2 * j), stacked(a, 2 * j + 1)
                    V.tensor_copy(second[0:P // 2, :], first[P // 2:P, :])
                    V.tensor_copy(second[P // 2:P, :], first[P // 2:P, :]).then_inc(s_s2, 1)
                    dve.wait_ge(s_s2, NH // 2 * a + j + 1)
                    V.tensor_copy(first[P // 2:P, :], first[0:P // 2, :]).then_inc(s_st, 1)

            def heads_out(n):
                dve.wait_ge(s_od, n + 1)
                m = n // 2
                if m >= 4 and n % 2 == 0:
                    dve.wait_ge(s_add[m % 4], 16 * (m // 4))
                v = ot[:, m % 4, :].rearrange("p (g h b) -> p h g b", g=NT, h=CPA)[:, CPQ * (n % 2):CPQ * (n % 2 + 1)]
                V.tensor_copy(v, ps_o[n % 2][:, :].rearrange("p (h g b) -> p h g b", h=CPQ, g=NT)).then_inc(s_oe, 1)

            conv_out(0)
            for n in range(C // 2):
                if n + 1 < C // 2:
                    conv_out(n + 1)
                conv_lo(n)
                if n == C // 2 - 3:
                    both_halves(0)
            for g in range(NT):
                dve.wait_ge(s_res[g], 32)
            both_halves(1)
            both_halves(2)
            for n in range(2 * NA * HQ):
                heads_out(n)
                if n % 2 == 1 and n // 2 + 3 < NA * HQ:
                    both_halves(n // 2 + 3)

        @block.tensor
        def _(pe):
            mm = nc.tensor.matmul

            def cond_first(n):
                pe.wait_ge(s_x[n], 16)
                pe.wait_ge(s_wbd, n + 1)
                if n >= SPLIT:
                    pe.wait_ge(s_xl, n - SPLIT + 1)
                for i in range(2):
                    m = 2 * n + i
                    if m >= 3:
                        pe.wait_ge(s_hg, m - 2)
                    if n < SPLIT:
                        mm(ps_h[m % 3][:, :], w_bd[:, n % (NG // 2), 2 * i:2 * i + 2, :], x_sb[:, n, :],
                           start=True, stop=True).then_inc(s_hd, 1)
                    else:
                        for w, v in ((0, 0), (1, 0), (0, 1)):
                            last = mm(ps_h[m % 3][:, :], w_part(n, w)[:, 2 * HID * i:2 * HID * (i + 1)], x_part(n, v),
                                      start=(w == v), stop=(v == 1))
                        last.then_inc(s_hd, 1)

            def cond_turned(n):
                pe.wait_ge(s_ct, n + 1)
                if n >= 2:
                    pe.wait_ge(s_cv, n - 1)
                if n == 2 * GPT:
                    pe.wait_ge(s_kf, 1)
                for k in range(KC):
                    last = nc.tensor.transpose(ps_c[n % 2][:, P * k:P * (k + 1)], c_t[:, n % 2, P * k:P * (k + 1)], ident[:, :])
                last.then_inc(s_tu, 1)

            def cond(g):
                for n in range(GPT * g, GPT * (g + 1)):
                    if n + 1 < NG:
                        cond_first(n + 1)
                    if n > GPT * g:
                        cond_turned(n - 1)
                    pe.wait_ge(s_hg, 2 * (n + 1))
                    if n == 0:
                        pe.wait_ge(s_w2, 32)
                    else:
                        pe.wait_ge(s_ct, n)
                    for i in range(2):
                        last = mm(ps_g[2 * C * i:2 * C * (i + 1), :], w2_bd[:, :], hid0[:, (2 * n + i) % 4, :],
                                  start=True, stop=True)
                    last.then_inc(s_hu, 1)

            pe.wait_ge(s_ohe, 1)
            for i in range(2):
                last = mm(ring("bias")[HID * i:HID * (i + 1), 0:B // 2], bs_sb[:, :], onehot_e[:, i, :], start=True, stop=True)
            filled(last, "bias")
            pe.wait_ge(s_idn, 2)
            cond_first(0)
            cond(0)
            cond_turned(GPT - 1)
            pe.wait_ge(s_wl, 1)

            def low_rank(g):
                for i in range(2):
                    if g == NT - 1:
                        acc = ps_h[i]
                        pe.wait_ge(s_hg, NG * 2)
                    else:
                        acc = ring(f"lr{g}{i}")
                        wait_free(pe, f"lr{g}{i}")
                    for s in range(2):
                        pe.wait_ge(s_cl, GPT * g + 2 * i + s + 1)
                        tok = slice(P * (2 * i + s), P * (2 * i + s + 1))
                        for k in range(KC):
                            for c, w in ((c0_hi, ar_hi), (c0_hi, ar_lo), (c0_lo, ar_hi)):
                                last = mm(acc[:, LR * s:LR * (s + 1)], c[:, g % 2, k, tok], w[:, k, :],
                                          start=(k == 0 and c is c0_hi and w is ar_hi), stop=(k == KC - 1 and c is c0_lo))
                    if g == NT - 1:
                        last.then_inc(s_lr3, 1)
                    else:
                        filled(last, f"lr{g}{i}")

            def low_rank_turned(g):
                if g == NT - 1:
                    pe.wait_ge(s_hw3, 2)
                else:
                    for i in range(2):
                        pe.wait_ge(s_ff[unit[f"lr{g}{i}"] % 2], unit[f"lr{g}{i}"] // 2 + 1)
                wait_free(pe, f"hw{g}")
                for s in range(GPT):
                    last = nc.tensor.transpose(ring(f"hw{g}")[:, P * s:P * (s + 1)], hw[:, s, :], ident[:, :])
                filled(last, f"hw{g}")

            def linear_base(g, i):
                acc = linear_bank(g, i)
                if i == 0:
                    pe.wait_ge(s_ct, min(GPT * (g + 2), NG))
                    if g >= 1:
                        pe.wait_ge(s_g0, g)
                else:
                    wait_free(pe, f"oc{g}{i}")
                for k in range(KC):
                    for w, c in ((wb_hi, c0_hi), (wb_hi, c0_lo), (wb_lo, c0_hi)):
                        mm(acc[:, :], w[:, k, P * i:P * (i + 1)], c[:, g % 2, k, :],
                           start=(k == 0 and w is wb_hi and c is c0_hi), stop=False, skip_group_check=True)

            def linear_lora(g, i):
                if i == 0:
                    pe.wait_ge(s_ff[unit[f"hw{g}"] % 2], unit[f"hw{g}"] // 2 + 1)
                for w, h in ((b_hi, hwt_hi), (b_hi, hwt_lo), (b_lo, hwt_hi)):
                    last = mm(linear_bank(g, i)[:, :], w[:, P * i:P * (i + 1)], h[:, :], start=False, stop=(w is b_lo),
                              skip_group_check=True)
                if i == 0:
                    last.then_inc(s_r0, 1)
                else:
                    filled(last, f"oc{g}{i}")

            for g in range(NT - 1):
                low_rank(g)
                cond(g + 1)
                if g == 0:
                    pe.wait_ge(s_wbl, 1)
                linear_base(g, 0)
                low_rank_turned(g)
                if g == NT - 2:
                    cond_turned(NG - 1)
                if g == 0:
                    pe.wait_ge(s_k4, 1)
                    pe.wait_ge(s_ke, 1)
                    pe.wait_ge(s_cv, 2 * GPT - 1)
                    for a in range(4):
                        last = nc.tensor.transpose(ps_c[0][:, C * a:C * (a + 1)],
                                                   k4[:, a, :, :].rearrange("h c n -> h (c n)"), ident[0:C, 0:C])
                    last.then_inc(s_k4p, 1)
                    pe.wait_ge(s_wl, 2)
                linear_base(g, 1)
                if g == NT - 2:
                    low_rank(NT - 1)
                linear_lora(g, 0)
                linear_lora(g, 1)
                if g < NT - 2:
                    cond_turned(GPT * (g + 2) - 1)
                if g == NT - 2:
                    pe.wait_ge(s_kt, 1)
                    pe.wait_ge(s_cv, NG)
                    for i in range(2):
                        for h in range(C // 2):
                            hh = C // 2 * i + h
                            last = mm(ps_c[i][0:NI, NJ * h:NJ * (h + 1)], coarse[:, hh, :], fine[:, hh, :], start=True, stop=True)
                        last.then_inc(s_kd, 1)
                for i in range(2, KC):
                    linear_base(g, i)
                    linear_lora(g, i)
            linear_base(NT - 1, 0)
            low_rank_turned(NT - 1)
            linear_base(NT - 1, 1)
            for i in range(2):
                linear_lora(NT - 1, i)
            for i in range(2, KC):
                linear_base(NT - 1, i)
                linear_lora(NT - 1, i)

            def conv(h):
                pe.wait_ge(s_tp[h // 4], 64)
                if h % 2 == 0 and h >= 4:
                    pe.wait_ge(s_yf, h // 2 - 1)
                acc = ps_y[(h // 2) % 2][:, KC * B * (h % 2):KC * B * (h % 2 + 1)]
                for part, v in ((0, u_hi), (1, u_hi), (0, u_lo)):
                    if h == 0 and v is u_lo:
                        pe.wait_ge(s_ul, NT * KC)
                    for d in range(KC):
                        block_d = slice(P * (KC - 1 - d), P * (KC - d))
                        last = mm(acc[:, B * d:KC * B], toep(h, part)[:, block_d], v[:, 0:KC - d, h, :],
                                  start=(d == 0 and part == 0 and v is u_hi), stop=(d == KC - 1 and v is u_lo),
                                  skip_group_check=True)
                last.then_inc(s_cd, 1)

            def rise(n):
                a, h, half = n // (2 * NH), n % (2 * NH) // 8 * 4 + n % 4, n % 8 // 4
                if n % 8 in (0, 2):
                    pe.wait_ge(s_st, NH // 2 * a + h // 2 + 1)
                if n == 4:
                    pe.wait_ge(s_yf, C // 2)
                if n >= 6 and n % 2 == 0:
                    pe.wait_ge(s_ug, n - 4)
                mm(ps_u[n // 2 % 3][:, n % 2, :], up_st[:, h, :], stacked(a, h)[:, TOK * half:TOK * (half + 1)],
                   start=True, stop=True).then_inc(s_ud, 1)

            def falls(n):
                q = n % (2 * HQ) // 2
                pe.wait_ge(s_ug, 4 * (n + 1))
                if n >= 2:
                    pe.wait_ge(s_oe, n - 1)
                for i in range(4):
                    last = mm(ps_o[n % 2][DH * i:DH * (i + 1), :], down_sb[:, 4 * q + i, :], hid1[:, (4 * n + i) % 8, :],
                              start=True, stop=True)
                last.then_inc(s_od, 1)

            pe.wait_ge(s_uf, NT * KC)
            for h in range(C):
                conv(h)
            pe.wait_ge(s_l1, 96)
            pe.wait_ge(s_up, 2)
            for n in range(4):
                rise(n)
            for n in range(NH):
                for i in range(4):
                    if 4 * (n + 1) + i < 4 * NH:
                        rise(4 * (n + 1) + i)
                falls(n)


def kernel(**inputs):
    import numpy as _np
    import concourse.bacc as _bacc
    from concourse import mybir as _mybir
    from concourse.bass_utils import run_bass_kernel_spmd as _run

    v = {name: _np.asarray(a) for name, a in inputs.items()}
    low = v["L0_ffn_A"].reshape(-1, v["L0_ffn_A"].shape[2])
    laid_out = {
        "x": v["x"],
        "x_steps": v["x"].reshape(4, -1, *v["x"].shape[1:]).transpose(0, 3, 2, 1),
        "sess_id": v["itok_B_0_7"],
        "sess_chan_by4": _np.concatenate([v["itok_B_0_7"].reshape(-1, 4).T, v["_lenS"].reshape(-1, 4).T], axis=1),
        "seq_len": v["itok_B_2182_4065"],
        "conv_len": v["itok_B_8_3872"],
        "w_sess": v["L0_cond_W_sess"],
        "b_sess": v["L0_cond_b_sess"],
        "w2": v["L0_cond_W2"],
        "b2": v["L0_cond_b2"],
        "w_base_t": v["L0_ffn_W_base"].T,
        "b_base_c": v["L0_ffn_b_base"].reshape(-1, 128).T,
        "low_router_t": _np.concatenate([low, v["L0_ffn_W_router"]]).T,
        "lora_b_t": v["L0_ffn_B"].transpose(0, 2, 1).reshape(low.shape[0], -1),
        "log_dt": v["L1_cond_log_dt"],
        "c_ri": v["L1_cond_C"],
        "log_a_re": v["L1_cond_log_A_real"],
        "a_im": v["L1_cond_A_imag"],
        "d_skip": v["L1_cond_D"],
        "up": v["L1_ffn_up"],
        "down": v["L1_ffn_down"],
        "perm_c": v["L1_ffn_perm"].reshape(-1, 128).T,
        "perm_h": v["L1_ffn_perm"].reshape(v["L1_ffn_up"].shape[0] // 2, 2, -1).transpose(1, 2, 0),
    }
    nc = _bacc.Bacc("TRN2", target_bir_lowering=False, num_devices=1)
    arrays, args = {}, []
    for name, a in laid_out.items():
        a = _np.ascontiguousarray(a)
        arrays[f"in_{name}"] = a
        args.append(nc.dram_tensor(f"in_{name}", a.shape, _mybir.dt.from_np(a.dtype), kind="ExternalInput").ap())
    batches, channels, steps = v["x"].shape
    res = nc.dram_tensor("out_dram", (2, steps, 4, channels // 2, batches // 4), _mybir.dt.float32, kind="ExternalOutput").ap()
    adaln_ffn_kernel(nc, *args, res)
    r = _run(nc, [arrays], core_ids=[0])
    return r.results[0]["out_dram"].transpose(2, 4, 0, 3, 1).reshape(batches, channels, steps)
```
